# Optimizing a Trainium2 kernel written in Bass

```python
import numpy as np
import jax
import jax.numpy as jnp

def _softmax(x, axis=-1):
    return jax.nn.softmax(x, axis=axis)

def _gelu(x):
    return jax.nn.gelu(x, approximate=True)

def _silu(x):
    return jax.nn.silu(x)

def _sigmoid(x):
    return jax.nn.sigmoid(x)

def _layernorm(x, axis=-1, eps=1e-05):
    m = jnp.mean(x, axis=axis, keepdims=True)
    v = jnp.var(x, axis=axis, keepdims=True)
    return (x - m) / jnp.sqrt(v + eps)

def _scatter_add(tgt, idx, src, axis=0):
    return tgt.at[idx].add(src)

def _segment_sum(src, seg, n):
    return jax.ops.segment_sum(src, seg, n)
kernel_name = 'mk_seq_preln_d2_jaxref_r8_2b5ba5'

def setup_inputs(seed: int=0):
    np.random.seed(seed)
    _w = jnp.asarray

    def _L0_attn_setup():
        import jax, jax.numpy as jnp
        import numpy as np
        B, N, D, H = (8, 512, 128, 16)
        HD = D // H
        EPS = 1e-05
        key = jax.random.key(seed)
        ks = jax.random.split(key, 18)
        s = 1.0 / np.sqrt(D)

        def lin(k):
            return (jax.random.normal(k, (D, D), jnp.float32) * s, jnp.zeros((D,), jnp.float32))
        Wg_w, Wg_b = lin(ks[0])
        Wr_w, Wr_b = lin(ks[1])
        Wk_w, Wk_b = lin(ks[2])
        Wv_w, Wv_b = lin(ks[3])
        Wo_w, Wo_b = lin(ks[4])
        mg = jax.random.uniform(ks[5], (D,), jnp.float32)
        mr = jax.random.uniform(ks[6], (D,), jnp.float32)
        mk = jax.random.uniform(ks[7], (D,), jnp.float32)
        mv = jax.random.uniform(ks[8], (D,), jnp.float32)
        w = jax.random.normal(ks[9], (H, HD), jnp.float32)
        u = jax.random.normal(ks[10], (H, HD), jnp.float32)
        x = jax.random.normal(ks[11], (B, N, D), jnp.float32)
        return {'x': x, 'Wg_w': Wg_w, 'Wg_b': Wg_b, 'Wr_w': Wr_w, 'Wr_b': Wr_b, 'Wk_w': Wk_w, 'Wk_b': Wk_b, 'Wv_w': Wv_w, 'Wv_b': Wv_b, 'Wo_w': Wo_w, 'Wo_b': Wo_b, 'mg': mg, 'mr': mr, 'mk': mk, 'mv': mv, 'w': w, 'u': u}
    _L0_attn_in = _L0_attn_setup()

    def _L0_ffn_setup():
        import jax, jax.numpy as jnp
        import numpy as np
        JITTER_EPS = 0.01

        def phi_routing(logits, jitter_eps=JITTER_EPS):
            m, sel = jax.lax.top_k(logits, 2)
            T, E = logits.shape
            m1 = m[:, :1]
            factor1 = jnp.maximum(jnp.abs(logits), m1)
            mask1 = (m1 - logits) / factor1 > 2.0 * jitter_eps
            p1 = jax.nn.softmax(jnp.where(mask1, -jnp.inf, logits), axis=-1)
            mult1 = jnp.take_along_axis(p1, sel[:, :1], axis=-1)
            m2 = m[:, 1:2]
            factor2 = jnp.maximum(jnp.abs(logits), m2)
            mask2 = (m2 - logits) / factor2 > 2.0 * jitter_eps
            drop_top1 = jnp.arange(E)[None, :] == sel[:, :1]
            p2 = jax.nn.softmax(jnp.where(mask2 | drop_top1, -jnp.inf, logits), axis=-1)
            mult2 = jnp.take_along_axis(p2, sel[:, 1:2], axis=-1)
            return (jnp.concatenate([mult1, mult2], axis=-1), sel)
        key = jax.random.key(seed)
        k = jax.random.split(key, 5)
        B, S, H, F, E = (1, 64, 128, 512, 8)
        return {'hidden_states': jax.random.normal(k[0], (B, S, H), jnp.float32), 'gate_w': jax.random.normal(k[1], (E, H), jnp.float32) * 0.02, 'w1': jax.random.normal(k[2], (E, F, H), jnp.float32) * 0.02, 'w2': jax.random.normal(k[3], (E, H, F), jnp.float32) * 0.02, 'w3': jax.random.normal(k[4], (E, F, H), jnp.float32) * 0.02}
    _L0_ffn_in = _L0_ffn_setup()

    def _L1_attn_setup():
        import jax, jax.numpy as jnp
        import numpy as np
        EPS = 1e-05

        def rwkv6_scan(q, k, v, w, u):
            B, H, T, K = q.shape
            V = v.shape[-1]
            h0 = jnp.zeros((B, H, K, V), jnp.float32)

            def step(h, xs):
                qi, ki, vi, wi = xs
                kv = ki[..., :, None] * vi[..., None, :]
                oi = jnp.einsum('bhk,bhkv->bhv', qi, h + u[None, :, :, None] * kv)
                h = h * jnp.exp(wi)[..., None] + kv
                return (h, oi)
            xs = tuple((jnp.moveaxis(a, 2, 0) for a in (q, k, v, w)))
            _, o = jax.lax.scan(step, h0, xs)
            return jnp.moveaxis(o, 0, 2)
        key = jax.random.key(seed)
        ks = jax.random.split(key, 20)
        B, T, D = (2, 256, 128)
        H, Dk, Dv = (4, 128, 32)
        KD, VD = (H * Dk, H * Dv)
        R5, LR = (5 * 32, 64)
        s = 0.02
        rn = lambda k, shp: jax.random.normal(k, shp, dtype=jnp.float32) * s
        return {'hidden_states': jax.random.normal(ks[0], (B, T, D), dtype=jnp.float32), 'xp_mu': rn(ks[1], (D,)), 'xp_W1': rn(ks[2], (R5, D)), 'xp_W2': rn(ks[3], (D, R5)), 'x_bias': rn(ks[4], (5, D)), 'r_W': rn(ks[5], (KD, D)), 'w_A': rn(ks[6], (LR, D)), 'w_B': rn(ks[7], (KD, LR)), 'w_b': rn(ks[8], (KD,)), 'k_W': rn(ks[9], (KD, D)), 'v_W': rn(ks[10], (VD, D)), 'g_A': rn(ks[11], (LR, D)), 'g_B': rn(ks[12], (VD, LR)), 'g_b': rn(ks[13], (VD,)), 'bonus': rn(ks[14], (H, Dk)), 'gn_w': jnp.ones((VD,), jnp.float32), 'gn_b': jnp.zeros((VD,), jnp.float32), 'o_W': rn(ks[15], (D, VD))}
    _L1_attn_in = _L1_attn_setup()

    def _L1_ffn_setup():
        import jax, jax.numpy as jnp
        import numpy as np
        BLOCK = 16
        _GRID = jnp.array([0.0, 0.5, 1.0, 1.5, 2.0, 3.0, 4.0, 6.0], dtype=jnp.float32)
        _MID = jnp.array([0.25, 0.75, 1.25, 1.75, 2.5, 3.5, 5.0], dtype=jnp.float32)

        def fp4_quant_dequant(x):
            shape = x.shape
            xb = x.reshape(shape[:-1] + (shape[-1] // BLOCK, BLOCK))
            scale = jnp.max(jnp.abs(xb), axis=-1, keepdims=True) / 6.0
            scale = jnp.maximum(scale, jnp.float32(1e-12))
            xn = xb / scale
            idx = jnp.searchsorted(_MID, jnp.abs(xn))
            q = _GRID[idx] * jnp.sign(xn) * scale
            return q.reshape(shape)

        def fp4_linear(x, w):
            xq = fp4_quant_dequant(x)
            wq = fp4_quant_dequant(w)
            return jnp.einsum('bsk,nk->bsn', xq, wq)
        key = jax.random.key(seed)
        k1, k2, k3, k4 = jax.random.split(key, 4)
        H, I = (128, 352)
        x = jax.random.normal(k1, (4, 512, H), dtype=jnp.float32)
        w_gate = jax.random.normal(k2, (I, H), dtype=jnp.float32) * 0.02
        w_up = jax.random.normal(k3, (I, H), dtype=jnp.float32) * 0.02
        w_down = jax.random.normal(k4, (H, I), dtype=jnp.float32) * 0.02
        return {'x': x, 'w_gate': w_gate, 'w_up': w_up, 'w_down': w_down}
    _L1_ffn_in = _L1_ffn_setup()
    _d = {'L0_attn_x': _L0_attn_in['x'], 'L0_attn_Wg_w': _L0_attn_in['Wg_w'], 'L0_attn_Wg_b': _L0_attn_in['Wg_b'], 'L0_attn_Wr_w': _L0_attn_in['Wr_w'], 'L0_attn_Wr_b': _L0_attn_in['Wr_b'], 'L0_attn_Wk_w': _L0_attn_in['Wk_w'], 'L0_attn_Wk_b': _L0_attn_in['Wk_b'], 'L0_attn_Wv_w': _L0_attn_in['Wv_w'], 'L0_attn_Wv_b': _L0_attn_in['Wv_b'], 'L0_attn_Wo_w': _L0_attn_in['Wo_w'], 'L0_attn_Wo_b': _L0_attn_in['Wo_b'], 'L0_attn_mg': _L0_attn_in['mg'], 'L0_attn_mr': _L0_attn_in['mr'], 'L0_attn_mk': _L0_attn_in['mk'], 'L0_attn_mv': _L0_attn_in['mv'], 'L0_attn_w': _L0_attn_in['w'], 'L0_attn_u': _L0_attn_in['u'], 'L0_ffn_gate_w': _L0_ffn_in['gate_w'], 'L0_ffn_w1': _L0_ffn_in['w1'], 'L0_ffn_w2': _L0_ffn_in['w2'], 'L0_ffn_w3': _L0_ffn_in['w3'], 'L1_attn_xp_mu': _L1_attn_in['xp_mu'], 'L1_attn_xp_W1': _L1_attn_in['xp_W1'], 'L1_attn_xp_W2': _L1_attn_in['xp_W2'], 'L1_attn_x_bias': _L1_attn_in['x_bias'], 'L1_attn_r_W': _L1_attn_in['r_W'], 'L1_attn_w_A': _L1_attn_in['w_A'], 'L1_attn_w_B': _L1_attn_in['w_B'], 'L1_attn_w_b': _L1_attn_in['w_b'], 'L1_attn_k_W': _L1_attn_in['k_W'], 'L1_attn_v_W': _L1_attn_in['v_W'], 'L1_attn_g_A': _L1_attn_in['g_A'], 'L1_attn_g_B': _L1_attn_in['g_B'], 'L1_attn_g_b': _L1_attn_in['g_b'], 'L1_attn_bonus': _L1_attn_in['bonus'], 'L1_attn_gn_w': _L1_attn_in['gn_w'], 'L1_attn_gn_b': _L1_attn_in['gn_b'], 'L1_attn_o_W': _L1_attn_in['o_W'], 'L1_ffn_w_gate': _L1_ffn_in['w_gate'], 'L1_ffn_w_up': _L1_ffn_in['w_up'], 'L1_ffn_w_down': _L1_ffn_in['w_down']}
    _x0 = _d['L0_attn_x']
    _d['L0_attn_x'] = jax.random.normal(jax.random.fold_in(jax.random.key(seed), 1), (16, 512, 128), dtype=_x0.dtype)
    del _x0
    return _d

def reference(L0_attn_x, L0_attn_Wg_w, L0_attn_Wg_b, L0_attn_Wr_w, L0_attn_Wr_b, L0_attn_Wk_w, L0_attn_Wk_b, L0_attn_Wv_w, L0_attn_Wv_b, L0_attn_Wo_w, L0_attn_Wo_b, L0_attn_mg, L0_attn_mr, L0_attn_mk, L0_attn_mv, L0_attn_w, L0_attn_u, L0_ffn_gate_w, L0_ffn_w1, L0_ffn_w2, L0_ffn_w3, L1_attn_xp_mu, L1_attn_xp_W1, L1_attn_xp_W2, L1_attn_x_bias, L1_attn_r_W, L1_attn_w_A, L1_attn_w_B, L1_attn_w_b, L1_attn_k_W, L1_attn_v_W, L1_attn_g_A, L1_attn_g_B, L1_attn_g_b, L1_attn_bonus, L1_attn_gn_w, L1_attn_gn_b, L1_attn_o_W, L1_ffn_w_gate, L1_ffn_w_up, L1_ffn_w_down):

    def _L0_attn_ref(x, Wg_w, Wg_b, Wr_w, Wr_b, Wk_w, Wk_b, Wv_w, Wv_b, Wo_w, Wo_b, mg, mr, mk, mv, w, u):
        import jax, jax.numpy as jnp
        import numpy as np
        B, N, D, H = (8, 512, 128, 16)
        HD = D // H
        EPS = 1e-05
        b, n, d = x.shape
        x_shift = jnp.roll(x, shift=1, axis=1)

        def mix(m, W, bias):
            return (m * x + (1.0 - m) * x_shift) @ W.T + bias
        g = mix(mg, Wg_w, Wg_b).reshape(b, n, H, HD)
        r = mix(mr, Wr_w, Wr_b).reshape(b, n, H, HD)
        k = mix(mk, Wk_w, Wk_b).reshape(b, n, H, HD)
        v = mix(mv, Wv_w, Wv_b).reshape(b, n, H, HD)
        kv = k * v
        decay = jnp.exp(-jnp.exp(w))
        kv_t = jnp.swapaxes(kv, 0, 1)

        def step(acc, kvt):
            acc = decay * acc + kvt
            return (acc, acc)
        _, accs = jax.lax.scan(step, jnp.zeros((b, H, HD), x.dtype), kv_t)
        wkv = jnp.swapaxes(accs, 0, 1) + u * kv
        rw = r * wkv
        mean = jnp.mean(rw, axis=-1, keepdims=True)
        var = jnp.var(rw, axis=-1, keepdims=True)
        ln = (rw - mean) * jax.lax.rsqrt(var + EPS)
        out = (jax.nn.sigmoid(g) * ln).reshape(b, n, d)
        return out @ Wo_w.T + Wo_b

    def _L0_ffn_ref(hidden_states, gate_w, w1, w2, w3):
        import jax, jax.numpy as jnp
        import numpy as np
        JITTER_EPS = 0.01

        def phi_routing(logits, jitter_eps=JITTER_EPS):
            m, sel = jax.lax.top_k(logits, 2)
            T, E = logits.shape
            m1 = m[:, :1]
            factor1 = jnp.maximum(jnp.abs(logits), m1)
            mask1 = (m1 - logits) / factor1 > 2.0 * jitter_eps
            p1 = jax.nn.softmax(jnp.where(mask1, -jnp.inf, logits), axis=-1)
            mult1 = jnp.take_along_axis(p1, sel[:, :1], axis=-1)
            m2 = m[:, 1:2]
            factor2 = jnp.maximum(jnp.abs(logits), m2)
            mask2 = (m2 - logits) / factor2 > 2.0 * jitter_eps
            drop_top1 = jnp.arange(E)[None, :] == sel[:, :1]
            p2 = jax.nn.softmax(jnp.where(mask2 | drop_top1, -jnp.inf, logits), axis=-1)
            mult2 = jnp.take_along_axis(p2, sel[:, 1:2], axis=-1)
            return (jnp.concatenate([mult1, mult2], axis=-1), sel)
        B, S, H = hidden_states.shape
        E = w1.shape[0]
        x = hidden_states.reshape(-1, H)
        logits = x @ gate_w.T
        routing_weights, selected = phi_routing(logits)
        T = x.shape[0]
        wte = jnp.zeros((T, E), x.dtype).at[jnp.arange(T)[:, None], selected].add(routing_weights)
        out = jnp.zeros_like(x)
        for e in range(E):
            h = jax.nn.silu(x @ w1[e].T) * (x @ w3[e].T)
            out = out + wte[:, e:e + 1] * (h @ w2[e].T)
        return out.reshape(B, S, H)

    def _L1_attn_ref(hidden_states, xp_mu, xp_W1, xp_W2, x_bias, r_W, w_A, w_B, w_b, k_W, v_W, g_A, g_B, g_b, bonus, gn_w, gn_b, o_W):
        import jax, jax.numpy as jnp
        import numpy as np
        EPS = 1e-05

        def rwkv6_scan(q, k, v, w, u):
            B, H, T, K = q.shape
            V = v.shape[-1]
            h0 = jnp.zeros((B, H, K, V), jnp.float32)

            def step(h, xs):
                qi, ki, vi, wi = xs
                kv = ki[..., :, None] * vi[..., None, :]
                oi = jnp.einsum('bhk,bhkv->bhv', qi, h + u[None, :, :, None] * kv)
                h = h * jnp.exp(wi)[..., None] + kv
                return (h, oi)
            xs = tuple((jnp.moveaxis(a, 2, 0) for a in (q, k, v, w)))
            _, o = jax.lax.scan(step, h0, xs)
            return jnp.moveaxis(o, 0, 2)
        B, T, D = hidden_states.shape
        H = bonus.shape[0]
        x = hidden_states
        shifted = jnp.pad(x, ((0, 0), (1, 0), (0, 0)))[:, :-1]
        delta = shifted - x
        xl = jnp.tanh((x + delta * xp_mu) @ xp_W1.T)
        xl = xl.reshape(B, T, 5, -1)
        W2 = xp_W2.reshape(D, 5, -1)
        x5 = jnp.einsum('blnr,hnr->blnh', xl, W2) + x_bias
        mur, muw, muk, muv, mug = (x5[:, :, i] for i in range(5))
        r = (x + delta * mur) @ r_W.T
        w = jnp.tanh((x + delta * muw) @ w_A.T) @ w_B.T + w_b
        k = (x + delta * muk) @ k_W.T
        v = (x + delta * muv) @ v_W.T
        g = jnp.tanh((x + delta * mug) @ g_A.T) @ g_B.T + g_b
        heads = lambda a: a.reshape(B, T, H, -1).transpose(0, 2, 1, 3)
        r, w, k, v = map(heads, (r, w, k, v))
        w = -jnp.exp(w)
        o = rwkv6_scan(r, k, v, w, bonus)
        o = o.transpose(0, 2, 1, 3).reshape(B, T, -1)
        mu = o.mean(-1, keepdims=True)
        var = ((o - mu) ** 2).mean(-1, keepdims=True)
        o = (o - mu) * jax.lax.rsqrt(var + EPS) * gn_w + gn_b
        o = o * (g * jax.nn.sigmoid(g))
        return o @ o_W.T

    def _L1_ffn_ref(x, w_gate, w_up, w_down):
        import jax, jax.numpy as jnp
        import numpy as np
        BLOCK = 16
        _GRID = jnp.array([0.0, 0.5, 1.0, 1.5, 2.0, 3.0, 4.0, 6.0], dtype=jnp.float32)
        _MID = jnp.array([0.25, 0.75, 1.25, 1.75, 2.5, 3.5, 5.0], dtype=jnp.float32)

        def fp4_quant_dequant(x):
            shape = x.shape
            xb = x.reshape(shape[:-1] + (shape[-1] // BLOCK, BLOCK))
            scale = jnp.max(jnp.abs(xb), axis=-1, keepdims=True) / 6.0
            scale = jnp.maximum(scale, jnp.float32(1e-12))
            xn = xb / scale
            idx = jnp.searchsorted(_MID, jnp.abs(xn))
            q = _GRID[idx] * jnp.sign(xn) * scale
            return q.reshape(shape)

        def fp4_linear(x, w):
            xq = fp4_quant_dequant(x)
            wq = fp4_quant_dequant(w)
            return jnp.einsum('bsk,nk->bsn', xq, wq)
        gate = fp4_linear(x, w_gate)
        y = fp4_linear(x, w_up)
        h = jax.nn.silu(gate) * y
        return fp4_linear(h, w_down)
    x = L0_attn_x
    x = x + _L0_attn_ref(_layernorm(x, axis=-1), L0_attn_Wg_w, L0_attn_Wg_b, L0_attn_Wr_w, L0_attn_Wr_b, L0_attn_Wk_w, L0_attn_Wk_b, L0_attn_Wv_w, L0_attn_Wv_b, L0_attn_Wo_w, L0_attn_Wo_b, L0_attn_mg, L0_attn_mr, L0_attn_mk, L0_attn_mv, L0_attn_w, L0_attn_u)
    x = x + _L0_ffn_ref(_layernorm(x, axis=-1), L0_ffn_gate_w, L0_ffn_w1, L0_ffn_w2, L0_ffn_w3)
    x = x + _L1_attn_ref(_layernorm(x, axis=-1), L1_attn_xp_mu, L1_attn_xp_W1, L1_attn_xp_W2, L1_attn_x_bias, L1_attn_r_W, L1_attn_w_A, L1_attn_w_B, L1_attn_w_b, L1_attn_k_W, L1_attn_v_W, L1_attn_g_A, L1_attn_g_B, L1_attn_g_b, L1_attn_bonus, L1_attn_gn_w, L1_attn_gn_b, L1_attn_o_W)
    x = x + _L1_ffn_ref(_layernorm(x, axis=-1), L1_ffn_w_gate, L1_ffn_w_up, L1_ffn_w_down)
    return x

_drawn_inputs = setup_inputs


def setup_inputs(seed=0):
    import zlib

    import numpy as np

    out = dict(_drawn_inputs(seed))
    spreads = {'L0_attn_Wg_b': (0.0, 0.405),
     'L0_attn_Wr_b': (0.0, 0.1),
     'L0_attn_Wk_b': (0.0, 0.1),
     'L0_attn_Wv_b': (0.0, 0.1),
     'L0_attn_Wo_b': (0.0, 0.1),
     'L1_attn_gn_w': (1.0, 0.6),
     'L1_attn_gn_b': (0.0, 0.8)}
    factors = {'L0_ffn_gate_w': 4.469,
     'L0_ffn_w1': 3.931,
     'L0_ffn_w2': 3.918,
     'L0_ffn_w3': 3.91,
     'L1_attn_xp_mu': 8.0,
     'L1_attn_xp_W1': 8.0,
     'L1_attn_xp_W2': 8.0,
     'L1_attn_x_bias': 8.0,
     'L1_attn_r_W': 8.0,
     'L1_attn_w_A': 8.0,
     'L1_attn_w_B': 8.0,
     'L1_attn_w_b': 8.0,
     'L1_attn_k_W': 8.0,
     'L1_attn_v_W': 8.0,
     'L1_attn_g_A': 8.0,
     'L1_attn_g_B': 8.0,
     'L1_attn_g_b': 8.0,
     'L1_attn_bonus': 8.0,
     'L1_attn_o_W': 8.0,
     'L1_ffn_w_gate': 6.563,
     'L1_ffn_w_up': 6.48,
     'L1_ffn_w_down': 6.508}
    for name, (base, spread) in spreads.items():
        noise = np.random.default_rng([zlib.crc32(name.encode()), seed]).standard_normal(out[name].shape)
        drawn = base * np.exp(spread * noise) if base else spread * noise
        out[name] = jnp.asarray(drawn.astype(out[name].dtype))
    for name, factor in factors.items():
        out[name] = (out[name] * factor).astype(out[name].dtype)
    return out
```

```python
from contextlib import ExitStack

import numpy as np

import concourse.bass as bass
from concourse import mybir

F32 = mybir.dt.float32
I32 = mybir.dt.int32
ALU = mybir.AluOpType
ACT = mybir.ActivationFunctionType
AX = mybir.AxisListType

P = 128
SEQS, SEQ = 16, 512
TOK = SEQS * SEQ
N = 512
EPS = 1e-5

E, F = 8, 512
FC = F // P
SUB = N // P
H, DK, DV = 4, 128, 32
C = 128
LEVELS = [1, 2, 4, 8, 16, 32, 64]
MIX, LR = 5, 64
I = 352
QB = 16
BIG = -3.0e38
MAGIC = 1.5 * 2.0 ** 22
SPLIT = 2.0 ** 22 + 1.0
NUDGE = 1.0 - 2.0 ** -24


def constants():
    eye = np.eye(P, dtype=np.float32)
    mean = np.full((P, P), 1.0 / P, np.float32)
    group = np.kron(np.eye(16), np.full((8, 8), 1.0 / 8)).astype(np.float32)
    j, i = np.arange(C)[:, None], np.arange(C)[None, :]
    masks = [((i // h) % 2 == 1) & (i // (2 * h) == j // (2 * h)) & ((j // h) % 2 == 0) for h in LEVELS]
    masks = np.stack(masks, 1).astype(np.int32)
    first = np.broadcast_to(np.arange(E, 0, -1, dtype=np.float32), (P, E))
    return {"c_eye": eye, "c_mean": mean, "c_center": eye - mean, "c_group": group,
            "c_gcenter": eye - group, "c_masks": masks, "c_first": np.ascontiguousarray(first)}


def broadcast(ap, axis, count):
    v = ap.unsqueeze(axis)
    shape = list(v.shape)
    shape[axis] = count
    return v.broadcast_to(shape)


def layernorm_phase(nc, name, x, xn, c_center, c_mean, eps):
    U = 4
    with ExitStack() as ctx:
        sem = lambda s: ctx.enter_context(nc.semaphore(f"{name}_{s}"))
        sb = lambda s, shape: ctx.enter_context(nc.sbuf_tensor(f"{name}_{s}", shape, F32))
        centered = [ctx.enter_context(nc.psum_tensor(f"{name}_centered{u}", [P, N], F32)) for u in range(U)]
        var = [ctx.enter_context(nc.psum_tensor(f"{name}_var{u}", [P, N], F32)) for u in range(U)]
        square = sb("square", [P, U, N])
        logvar = sb("logvar", [P, U, N])
        rstd = sb("rstd", [P, U, N])
        centered_ready, square_ready, var_ready = sem("centered"), sem("square"), sem("var")
        log_ready, rstd_ready, normed = sem("log"), sem("rstd"), sem("normed")
        block = ctx.enter_context(nc.Block())

        @block.tensor
        def _(pe):
            with pe.Fori(0, TOK // (U * N)) as i:
                for u in range(U):
                    pe.wait_ge(normed, i * U + u + 1)
                    nc.tensor.matmul(centered[u][:], c_center[:], x[:, bass.ds(i * (U * N) + u * N, N)],
                                     start=True, stop=True).then_inc(centered_ready, 1)
                for u in range(U):
                    pe.wait_ge(square_ready, i * U + u + 1)
                    nc.tensor.matmul(var[u][:], c_mean[:], square[:, u, :], start=True, stop=True).then_inc(var_ready, 1)

        @block.scalar
        def _(act):
            with act.Fori(0, TOK // (U * N)) as i:
                for u in range(U):
                    act.wait_ge(centered_ready, i * U + u + 1)
                    nc.scalar.activation(square[:, u, :], centered[u][:], ACT.Square).then_inc(square_ready, 1)
                for u in range(U):
                    act.wait_ge(var_ready, i * U + u + 1)
                    nc.scalar.activation(logvar[:, u, :], var[u][:], ACT.Ln, bias=eps[:, 0:1]).then_inc(log_ready, 1)
                for u in range(U):
                    act.wait_ge(log_ready, i * U + u + 1)
                    act.wait_ge(normed, i * U + u + 1)
                    nc.scalar.activation(rstd[:, u, :], logvar[:, u, :], ACT.Exp, scale=-0.5).then_inc(rstd_ready, 1)

        @block.vector
        def _(dve):
            dve.sem_inc(normed, U)
            with dve.Fori(0, TOK // (U * N)) as i:
                for u in range(U):
                    dve.wait_ge(rstd_ready, i * U + u + 1)
                    nc.vector.tensor_tensor(xn[:, bass.ds(i * (U * N) + u * N, N)], centered[u][:], rstd[:, u, :],
                                            ALU.mult).then_inc(normed, 1)


def build(nc, d, out):
    with ExitStack() as ctx:
        sb = lambda s, shape, dt=F32: ctx.enter_context(nc.sbuf_tensor(s, shape, dt))
        x = sb("x", [P, TOK])
        eye, mean, center = sb("eye", [P, P]), sb("mean", [P, P]), sb("center", [P, P])
        group, gcenter = sb("group", [P, P]), sb("gcenter", [P, P])
        eps = sb("eps", [P, 1])
        loaded = ctx.enter_context(nc.semaphore("loaded"))
        eps_set = ctx.enter_context(nc.semaphore("eps_set"))
        pairs = [(eye, "c_eye"), (mean, "c_mean"), (center, "c_center"), (group, "c_group"), (gcenter, "c_gcenter")]
        with nc.Block() as block:
            @block.sync
            def _(sp):
                for t, name in pairs:
                    sp.dma_start(t[:], d[name]).then_inc(loaded, 16)
                for q in range(4):
                    sp.dma_start(x[:, q * TOK // 4:(q + 1) * TOK // 4],
                                 d["x"][:, q * TOK // 4:(q + 1) * TOK // 4]).then_inc(loaded, 16)
                sp.wait_ge(loaded, 16 * (len(pairs) + 4))

            @block.gpsimd
            def _(pool):
                nc.gpsimd.memset(eps[:], EPS).then_inc(eps_set, 1)
                pool.wait_ge(eps_set, 1)
        with nc.sbuf_tensor("xn0", [P, TOK], F32) as xn, nc.sbuf_tensor("wte", [P, TOK // P, E], F32) as wte:
            layernorm_phase(nc, "ln0", x, xn, center, mean, eps)
            mix_attention_phase(nc, d, x, xn, gcenter, group, eps)
            layernorm_phase(nc, "ln1", x, xn, center, mean, eps)
            moe_route_phase(nc, d, xn, wte)
            moe_dense_phase(nc, d, x, xn, wte, eye)
        rwkv_phase(nc, d, x, center, mean, eye, eps)
        with nc.sbuf_tensor("xn1", [P, TOK], F32) as xn:
            layernorm_phase(nc, "ln3", x, xn, center, mean, eps)
            fp4_ffn_phase(nc, d, x, xn, eye)
        stored = ctx.enter_context(nc.semaphore("stored"))
        with nc.Block() as block:
            @block.sync
            def _(sp):
                for q in range(4):
                    sp.dma_start(out[:, q * TOK // 4:(q + 1) * TOK // 4],
                                 x[:, q * TOK // 4:(q + 1) * TOK // 4]).then_inc(stored, 16)
                sp.wait_ge(stored, 64)


def mix_attention_phase(nc, d, x, xn, gcenter, group, eps):
    U = 2
    names = ["k", "v", "g", "r"]
    with ExitStack() as ctx:
        sem = lambda s: ctx.enter_context(nc.semaphore(f"l0a_{s}"))
        sb = lambda s, shape: ctx.enter_context(nc.sbuf_tensor(f"l0a_{s}", shape, F32))
        bank = [[ctx.enter_context(nc.psum_tensor(f"l0a_bank{u}{b}", [P, N], F32)) for b in range(4)] for u in range(U)]
        W = sb("W", [P, 5, P])
        cols = sb("cols", [P, 11])
        mk, mv, mg, mr, bk, bv, bg, br, bo, w, u_ = [cols[:, j:j + 1] for j in range(11)]
        mm1 = sb("mm1", [P, 4])
        hbg = sb("hbg", [P, 1])
        ew, dec = sb("ew", [P, 1]), sb("dec", [P, 1])
        decay = sb("decay", [P, N])
        diff = sb("diff", [P, U, N])
        mix = sb("mix", [P, U, 4, N])
        k, th, kv, wkv, rw = (sb(s, [P, U, N]) for s in ("k", "th", "kv", "wkv", "rw"))
        acc = sb("acc", [P, U, N])
        square, logvar, rstd, gate, o = (sb(s, [P, U, N]) for s in ("square", "logvar", "rstd", "gate", "o"))
        loaded, prepared, ew_ready, dec_ready = sem("loaded"), sem("prepared"), sem("ew"), sem("dec")
        diff_ready, mixed = sem("diff"), sem("mixed")
        projected = {s: sem(f"proj_{s}") for s in names}
        k_ready, th_ready, kv_ready, acc_ready, wkv_ready = sem("k"), sem("th"), sem("kv"), sem("acc"), sem("wkv")
        rw_ready, centered_ready, square_ready, var_ready = sem("rw"), sem("centered"), sem("square"), sem("var")
        log_ready, rstd_ready, gate_ready, o_ready = sem("log"), sem("rstd"), sem("gate"), sem("o")
        out_ready, x_added = sem("out"), sem("x_added")
        vecs = ["L0_attn_mk", "L0_attn_mv", "L0_attn_mg", "L0_attn_mr", "L0_attn_Wk_b", "L0_attn_Wv_b",
                "L0_attn_Wg_b", "L0_attn_Wr_b", "L0_attn_Wo_b", "L0_attn_w", "L0_attn_u"]
        block = ctx.enter_context(nc.Block())
        ROUNDS = SEQS // U

        @block.sync
        def _(sp):
            for j, s in enumerate(["Wk_w", "Wv_w", "Wg_w", "Wr_w", "Wo_w"]):
                sp.dma_start(W[:, j, :], d["L0_attn_" + s]).then_inc(loaded, 16)
            for j, s in enumerate(vecs):
                sp.dma_start(cols[:, j:j + 1], d[s]).then_inc(loaded, 16)
            sp.wait_ge(loaded, 256)

        @block.tensor
        def _(pe):
            pe.wait_ge(loaded, 256)
            with pe.Fori(0, ROUNDS) as i:
                for j, s in enumerate(names):
                    for u in range(U):
                        n = i * U + u + 1
                        pe.wait_ge(mixed, i * (4 * U) + j * U + u + 1)
                        if s == "g":
                            pe.wait_ge(x_added, n)
                        nc.tensor.matmul(bank[u][j][:], W[:, j, :], mix[:, u, j, :], start=True,
                                         stop=True).then_inc(projected[s], 1)
                for u in range(U):
                    n = i * U + u + 1
                    pe.wait_ge(rw_ready, n)
                    pe.wait_ge(k_ready, n)
                    nc.tensor.matmul(bank[u][0][:], gcenter[:], rw[:, u, :], start=True,
                                     stop=True).then_inc(centered_ready, 1)
                for u in range(U):
                    n = i * U + u + 1
                    pe.wait_ge(square_ready, n)
                    nc.tensor.matmul(bank[u][1][:], group[:], square[:, u, :], start=True,
                                     stop=True).then_inc(var_ready, 1)
                for u in range(U):
                    n = i * U + u + 1
                    pe.wait_ge(o_ready, n)
                    nc.tensor.matmul(bank[u][2][:], W[:, 4, :], o[:, u, :], start=True, stop=True).then_inc(out_ready, 1)

        @block.scalar
        def _(act):
            act.wait_ge(loaded, 256)
            act.wait_ge(prepared, 2)
            nc.scalar.activation(ew[:], w, ACT.Exp).then_inc(ew_ready, 1)
            act.wait_ge(ew_ready, 1)
            nc.scalar.activation(dec[:], ew[:], ACT.Exp, scale=-1.0).then_inc(dec_ready, 1)
            with act.Fori(0, ROUNDS) as i:
                for u in range(U):
                    n = i * U + u + 1
                    act.wait_ge(projected["k"], n)
                    nc.scalar.activation(k[:, u, :], bank[u][0][:], ACT.Identity, bias=bk).then_inc(k_ready, 1)
                for u in range(U):
                    n = i * U + u + 1
                    act.wait_ge(projected["g"], n)
                    nc.scalar.activation(th[:, u, :], bank[u][2][:], ACT.Tanh, bias=hbg[:, 0:1],
                                         scale=0.5).then_inc(th_ready, 1)
                for u in range(U):
                    n = i * U + u + 1
                    act.wait_ge(centered_ready, n)
                    nc.scalar.activation(square[:, u, :], bank[u][0][:], ACT.Square).then_inc(square_ready, 1)
                for u in range(U):
                    n = i * U + u + 1
                    act.wait_ge(var_ready, n)
                    nc.scalar.activation(logvar[:, u, :], bank[u][1][:], ACT.Ln, bias=eps[:, 0:1]).then_inc(log_ready, 1)
                for u in range(U):
                    n = i * U + u + 1
                    act.wait_ge(log_ready, n)
                    nc.scalar.activation(rstd[:, u, :], logvar[:, u, :], ACT.Exp, scale=-0.5).then_inc(rstd_ready, 1)

        @block.vector
        def _(dve):
            dve.wait_ge(loaded, 256)
            nc.vector.tensor_scalar(mm1[:], cols[:, 0:4], -1.0, None, ALU.add).then_inc(prepared, 1)
            nc.vector.tensor_scalar(hbg[:], bg, 0.5, None, ALU.mult).then_inc(prepared, 1)
            dve.wait_ge(dec_ready, 1)
            nc.vector.tensor_copy(decay[:], dec[:, 0:1].broadcast_to([P, N])).then_inc(prepared, 1)
            dve.sem_inc(x_added, U)
            dve.wait_ge(prepared, 3)
            with dve.Fori(0, ROUNDS) as i:
                for u in range(U):
                    at = i * (U * N) + u * N
                    nc.vector.tensor_tensor(diff[:, u, 1:N], xn[:, bass.ds(at + 1, N - 1)], xn[:, bass.ds(at, N - 1)],
                                            ALU.subtract).then_inc(diff_ready, 1)
                    nc.vector.tensor_tensor(diff[:, u, 0:1], xn[:, bass.ds(at, 1)], xn[:, bass.ds(at + N - 1, 1)],
                                            ALU.subtract).then_inc(diff_ready, 1)
                for j in range(4):
                    for u in range(U):
                        dve.wait_ge(diff_ready, i * (2 * U) + 2 * u + 2)
                        nc.vector.scalar_tensor_tensor(mix[:, u, j, :], diff[:, u, :], mm1[:, j:j + 1],
                                                       xn[:, bass.ds(i * (U * N) + u * N, N)], ALU.mult,
                                                       ALU.add).then_inc(mixed, 1)
                for u in range(U):
                    n = i * U + u + 1
                    dve.wait_ge(projected["v"], n)
                    dve.wait_ge(k_ready, n)
                    nc.vector.scalar_tensor_tensor(kv[:, u, :], bank[u][1][:], bv, k[:, u, :], ALU.add,
                                                   ALU.mult).then_inc(kv_ready, 1)
                for u in range(U):
                    n = i * U + u + 1
                    dve.wait_ge(kv_ready, n)
                    nc.vector.tensor_tensor_scan(acc[:, u, :], decay[:], kv[:, u, :], 0.0, ALU.mult,
                                                 ALU.add).then_inc(acc_ready, 1)
                for u in range(U):
                    n = i * U + u + 1
                    dve.wait_ge(acc_ready, n)
                    nc.vector.scalar_tensor_tensor(wkv[:, u, :], kv[:, u, :], u_, acc[:, u, :], ALU.mult,
                                                   ALU.add).then_inc(wkv_ready, 1)
                for u in range(U):
                    n = i * U + u + 1
                    dve.wait_ge(wkv_ready, n)
                    dve.wait_ge(projected["r"], n)
                    nc.vector.scalar_tensor_tensor(rw[:, u, :], bank[u][3][:], br, wkv[:, u, :], ALU.add,
                                                   ALU.mult).then_inc(rw_ready, 1)
                for u in range(U):
                    n = i * U + u + 1
                    dve.wait_ge(rstd_ready, n)
                    dve.wait_ge(th_ready, n)
                    nc.vector.scalar_tensor_tensor(gate[:, u, :], th[:, u, :], 1.0, rstd[:, u, :], ALU.add,
                                                   ALU.mult).then_inc(gate_ready, 1)
                for u in range(U):
                    n = i * U + u + 1
                    dve.wait_ge(gate_ready, n)
                    nc.vector.scalar_tensor_tensor(o[:, u, :], bank[u][0][:], 0.5, gate[:, u, :], ALU.mult,
                                                   ALU.mult).then_inc(o_ready, 1)
                for u in range(U):
                    n = i * U + u + 1
                    at = i * (U * N) + u * N
                    dve.wait_ge(out_ready, n)
                    nc.vector.scalar_tensor_tensor(x[:, bass.ds(at, N)], bank[u][2][:], bo, x[:, bass.ds(at, N)],
                                                   ALU.add, ALU.add).then_inc(x_added, 1)


def moe_route_phase(nc, d, xn, wte):
    G = TOK // P
    with ExitStack() as ctx:
        sem = lambda s: ctx.enter_context(nc.semaphore(f"route_{s}"))
        sb = lambda s, shape: ctx.enter_context(nc.sbuf_tensor(f"route_{s}", shape, F32))
        gate_w, first = sb("gate_w", [P, E]), sb("first", [P, E])
        scores = ctx.enter_context(nc.psum_tensor("route_scores", [P, G, E], F32))
        L, L2, s1, s2, s3, one1, keep = (sb(s, [P, G, E]) for s in ("L", "L2", "s1", "s2", "s3", "one1", "keep"))
        m1, m2, r, t = (sb(s, [P, G]) for s in ("m1", "m2", "r", "t"))
        loaded, scored, step, exped = sem("loaded"), sem("scored"), sem("step"), sem("exped")
        block = ctx.enter_context(nc.Block())
        over = lambda v: broadcast(v[:], 2, E)
        firstb = broadcast(first[:], 1, G)

        @block.sync
        def _(sp):
            sp.dma_start(gate_w[:], d["L0_ffn_gate_w"]).then_inc(loaded, 16)
            sp.dma_start(first[:], d["c_first"]).then_inc(loaded, 16)
            sp.wait_ge(loaded, 32)

        @block.tensor
        def _(pe):
            pe.wait_ge(loaded, 32)
            for g in range(G):
                last = nc.tensor.matmul(scores[:, g, :], xn[:, g * P:(g + 1) * P], gate_w[:], start=True, stop=True)
            last.then_inc(scored, 1)

        @block.scalar
        def _(act):
            act.wait_ge(step, 7)
            nc.scalar.activation(s1[:], s1[:], ACT.Exp).then_inc(exped, 1)
            act.wait_ge(step, 22)
            nc.scalar.activation(s1[:], s1[:], ACT.Exp).then_inc(exped, 1)

        @block.vector
        def _(dve):
            count = [0]

            def then(ins):
                ins.then_inc(step, 1)
                count[0] += 1
                dve.wait_ge(step, count[0])

            TT, TS, STT = nc.vector.tensor_tensor, nc.vector.tensor_scalar, nc.vector.scalar_tensor_tensor
            dve.wait_ge(loaded, 32)
            dve.wait_ge(scored, 1)
            then(nc.vector.tensor_copy(L[:], scores[:]))
            then(nc.vector.tensor_reduce(m1[:], L[:], AX.X, ALU.max))
            then(TT(s2[:], L[:], over(m1), ALU.is_equal))
            then(TT(s2[:], s2[:], firstb, ALU.mult))
            then(nc.vector.tensor_reduce(r[:], s2[:], AX.X, ALU.max))
            then(TT(one1[:], s2[:], over(r), ALU.is_equal))
            then(TT(s1[:], L[:], over(m1), ALU.subtract))
            then(STT(s2[:], L[:], -1.0, L[:], ALU.mult, ALU.max))
            then(TT(s2[:], s2[:], over(m1), ALU.max))
            then(TT(s3[:], over(m1), L[:], ALU.subtract))
            then(STT(keep[:], s2[:], 0.02, s3[:], ALU.mult, ALU.is_ge))
            dve.wait_ge(exped, 1)
            then(TT(s2[:], s1[:], keep[:], ALU.mult))
            then(nc.vector.tensor_reduce(t[:], s2[:], AX.X, ALU.add))
            then(nc.vector.reciprocal(t[:], t[:]))
            then(TT(wte[:], one1[:], over(t), ALU.mult))
            then(STT(L2[:], one1[:], BIG, L[:], ALU.mult, ALU.add))
            then(nc.vector.tensor_reduce(m2[:], L2[:], AX.X, ALU.max))
            then(TT(s2[:], L2[:], over(m2), ALU.is_equal))
            then(TT(s2[:], s2[:], firstb, ALU.mult))
            then(nc.vector.tensor_reduce(r[:], s2[:], AX.X, ALU.max))
            then(TT(one1[:], s2[:], over(r), ALU.is_equal))
            then(TT(s1[:], L2[:], over(m2), ALU.subtract))
            then(STT(s2[:], L2[:], -1.0, L2[:], ALU.mult, ALU.max))
            then(TT(s2[:], s2[:], over(m2), ALU.max))
            then(TT(s3[:], over(m2), L2[:], ALU.subtract))
            then(STT(keep[:], s2[:], 0.02, s3[:], ALU.mult, ALU.is_ge))
            dve.wait_ge(exped, 2)
            then(TT(s2[:], s1[:], keep[:], ALU.mult))
            then(nc.vector.tensor_reduce(t[:], s2[:], AX.X, ALU.add))
            then(nc.vector.reciprocal(t[:], t[:]))
            then(TT(s2[:], one1[:], over(t), ALU.mult))
            then(TT(wte[:], wte[:], s2[:], ALU.add))


def moe_dense_phase(nc, d, x, xn, wte, eye):
    Q = E * FC
    with ExitStack() as ctx:
        sem = lambda s: ctx.enter_context(nc.semaphore(f"moe_{s}"))
        sb = lambda s, shape: ctx.enter_context(nc.sbuf_tensor(f"moe_{s}", shape, F32))
        w1, w3, w2 = sb("w1", [P, E, F]), sb("w3", [P, E, F]), sb("w2", [P, E, FC, P])
        silu, h = sb("silu", [P, 2, N]), sb("h", [P, 2, N])
        weight = sb("weight", [P, SUB, E])
        acc = sb("acc", [P, SUB, P])
        b1 = [ctx.enter_context(nc.psum_tensor(f"moe_b1{u}", [P, N], F32)) for u in range(2)]
        b3 = [ctx.enter_context(nc.psum_tensor(f"moe_b3{u}", [P, N], F32)) for u in range(2)]
        y = [ctx.enter_context(nc.psum_tensor(f"moe_y{u}", [P, SUB, P], F32)) for u in range(2)]
        yT = ctx.enter_context(nc.psum_tensor("moe_yT", [P, SUB, P], F32))
        loaded, gated, upped, silu_ready, h_ready = sem("loaded"), sem("gated"), sem("upped"), sem("silu"), sem("h")
        y_ready, y_added, weight_ready, turned, x_added = sem("y"), sem("y_added"), sem("weight"), sem("turned"), sem("x_added")
        block = ctx.enter_context(nc.Block())

        @block.sync
        def _(sp):
            sp.dma_start(w1[:], d["L0_ffn_w1"]).then_inc(loaded, 16)
            sp.dma_start(w3[:], d["L0_ffn_w3"]).then_inc(loaded, 16)
            sp.dma_start(w2[:], d["L0_ffn_w2"]).then_inc(loaded, 16)
            sp.wait_ge(loaded, 48)

        @block.tensor
        def _(pe):
            pe.wait_ge(loaded, 48)
            with pe.Fori(0, TOK // N) as i:
                def down(q):
                    e, c = divmod(q, FC)
                    pe.wait_ge(h_ready, i * Q + q + 1)
                    if c == 0:
                        pe.wait_ge(y_added, i * E + e + 1)
                    for t in range(SUB):
                        last = nc.tensor.matmul(y[e % 2][:, t, :], h[:, q % 2, t * P:(t + 1) * P], w2[:, e, c, :],
                                                start=(c == 0 and t == 0), stop=(c == FC - 1),
                                                skip_group_check=True)
                    last.then_inc(y_ready, 1)

                xt = xn[:, bass.ds(i * N, N)]
                for q in range(Q):
                    e, c = divmod(q, FC)
                    pe.wait_ge(silu_ready, i * Q + q + 1)
                    nc.tensor.matmul(b1[q % 2][:], w1[:, e, c * P:(c + 1) * P], xt, start=True, stop=True).then_inc(gated, 1)
                    if q >= 2:
                        pe.wait_ge(h_ready, i * Q + q - 1)
                    nc.tensor.matmul(b3[q % 2][:], w3[:, e, c * P:(c + 1) * P], xt, start=True, stop=True).then_inc(upped, 1)
                    if q:
                        down(q - 1)
                down(Q - 1)
                pe.wait_ge(y_added, i * E + E + 2)
                for t in range(SUB):
                    last = nc.tensor.transpose(yT[:, t, :], acc[:, t, :], eye[:])
                last.then_inc(turned, 1)

        @block.scalar
        def _(act):
            act.sem_inc(silu_ready, 2)
            with act.Fori(0, TOK // N) as i:
                for q in range(Q):
                    act.wait_ge(gated, i * Q + q + 1)
                    if q >= 2:
                        act.wait_ge(h_ready, i * Q + q - 1)
                    nc.scalar.activation(silu[:, q % 2, :], b1[q % 2][:], ACT.Silu).then_inc(silu_ready, 1)

        @block.vector
        def _(dve):
            dve.sem_inc(y_added, 2)
            with dve.Fori(0, TOK // N) as i:
                nc.vector.tensor_copy(weight[:], wte[:, bass.ds(i * SUB, SUB), :]).then_inc(weight_ready, 1)
                for q in range(Q + 1):
                    if q < Q:
                        dve.wait_ge(silu_ready, i * Q + q + 3)
                        dve.wait_ge(upped, i * Q + q + 1)
                        if q >= 2:
                            dve.wait_ge(y_ready, i * Q + q - 1)
                        nc.vector.tensor_tensor(h[:, q % 2, :], b3[q % 2][:], silu[:, q % 2, :],
                                                ALU.mult).then_inc(h_ready, 1)
                    if q and q % FC == 0:
                        e = q // FC - 1
                        dve.wait_ge(y_ready, i * Q + q)
                        dve.wait_ge(weight_ready, i + 1)
                        for t in range(SUB):
                            if e == 0:
                                last = nc.vector.tensor_scalar(acc[:, t, :], y[e % 2][:, t, :],
                                                               weight[:, t, e:e + 1], None, ALU.mult)
                            else:
                                if t == 0:
                                    dve.wait_ge(y_added, i * E + e + 2)
                                last = nc.vector.scalar_tensor_tensor(acc[:, t, :], y[e % 2][:, t, :],
                                                                      weight[:, t, e:e + 1], acc[:, t, :],
                                                                      ALU.mult, ALU.add)
                        last.then_inc(y_added, 1)
                dve.wait_ge(turned, i + 1)
                xt = x[:, bass.ds(i * N, N)]
                nc.vector.tensor_tensor(xt, yT[:].rearrange("p t c -> p (t c)"), xt, ALU.add).then_inc(x_added, 1)


def rwkv_phase(nc, d, x, center, mean, eye, eps):
    U = 2
    T = SEQ // C
    TH = T * H
    ROUNDS = SEQS // U
    NL = len(LEVELS)
    with ExitStack() as ctx:
        sem = lambda s: ctx.enter_context(nc.semaphore(f"l1a_{s}"))
        sb = lambda s, shape, dt=F32: ctx.enter_context(nc.sbuf_tensor(f"l1a_{s}", shape, dt))
        bank = [[ctx.enter_context(nc.psum_tensor(f"l1a_bank{u}{b}", [P, N], F32)) for b in range(4)] for u in range(U)]
        w1, w2a, w2b = sb("w1", [P, MIX * 32]), sb("w2a", [P, P]), sb("w2b", [32, P])
        rW, kW, vW, oW = sb("rW", [P, H, DK]), sb("kW", [P, H, DK]), sb("vW", [P, P]), sb("oW", [P, P])
        wA, wB, gA, gB = sb("wA", [P, LR]), sb("wB", [LR, H, DK]), sb("gA", [P, LR]), sb("gB", [LR, P])
        cols = sb("cols", [P, 17])
        x_bias, w_b, bonus = cols[:, 0:5], cols[:, 5:9], cols[:, 9:13]
        mu, g_b, gn_w, gn_b = (cols[:, j:j + 1] for j in range(13, 17))
        half_gb = sb("half_gb", [P, 1])
        masks = sb("masks", [P, NL, C], I32)
        square, logvar, rstd = (sb(s, [P, U, N]) for s in ("square", "logvar", "rstd"))
        xn, delta, scaled, z_last = (sb(s, [P, U, N]) for s in ("xn", "delta", "scaled", "z_last"))
        low, low4, lowrank = sb("low", [P, U, N]), sb("low4", [32, U, N]), sb("lowrank", [LR, U, N])
        q, k, decay, uq, S = (sb(s, [P, U, T, H, C]) for s in ("q", "k", "decay", "uq", "S"))
        v = sb("v", [P, U, T, P])
        state = sb("state", [P, U, T - 1, H, DV])
        g, silu_g, o = (sb(s, [P, U, N]) for s in ("g", "silu_g", "o"))
        flat = lambda t, u: t[:, u, :, :, :].rearrange("p t h c -> p (t h c)")
        z = lambda u, m: flat(S, u)[:, m * N:(m + 1) * N] if m < 4 else z_last[:, u, :]
        kT = uq

        def halves(t, u, h):
            return flat(t, u).rearrange("p (n two h) -> p n two h", two=2, h=h)

        loaded, prepared = sem("loaded"), sem("prepared")
        centered_ready, square_ready, var_ready, log_ready, rstd_ready = (
            sem(s) for s in ("centered", "square", "var", "log", "rstd"))
        xn_ready, delta_ready, z0_ready = sem("xn"), sem("delta"), sem("z0")
        low_mm, low4_mm, low_ready, low4_ready, x5_ready = sem("low_mm"), sem("low4_mm"), sem("low"), sem("low4"), sem("x5")
        mix_scaled, mix_ready = sem("mix_scaled"), sem("mix")
        r_mm, q_ready, uq_ready, k_mm, k_ready = sem("r_mm"), sem("q"), sem("uq"), sem("k_mm"), sem("k")
        wA_mm, wA_ready, wB_mm, exp_ready, decay_ready = sem("wA_mm"), sem("wA"), sem("wB_mm"), sem("exp"), sem("decay")
        v_mm, v_ready, gA_mm, gA_ready, gB_mm, g_ready, silu_ready = (
            sem(s) for s in ("v_mm", "v", "gA_mm", "gA", "gB_mm", "g", "silu"))
        diag_mm, diag_ready, level_mm, merged = sem("diag_mm"), sem("diag"), sem("level_mm"), sem("merged")
        q_scaled, k_scaled, total_ready = sem("q_scaled"), sem("k_scaled"), sem("total")
        turned, kT_ready, kv_mm, state_step = sem("turned"), sem("kT"), sem("kv_mm"), sem("state")
        o_mm, o_ready, oc_mm, osquare_ready, ovar_mm, olog_ready, orstd_ready = (
            sem(s) for s in ("o_mm", "o", "oc_mm", "osquare", "ovar_mm", "olog", "orstd"))
        o_step, out_mm, x_added = sem("o_step"), sem("out_mm"), sem("x_added")
        loads = [(w1[:], "xp_W1"), (w2a[:], "xp_W2a"), (w2b[:], "xp_W2b"), (rW[:], "r_W"), (kW[:], "k_W"),
                 (vW[:], "v_W"), (oW[:], "o_W"), (wA[:], "w_A"), (wB[:], "w_B"), (gA[:], "g_A"), (gB[:], "g_B"),
                 (x_bias, "x_bias"), (w_b, "w_b"), (bonus, "bonus"), (mu, "xp_mu"), (g_b, "g_b"),
                 (gn_w, "gn_w"), (gn_b, "gn_b")]
        LOADED = 16 * (len(loads) + 1)
        block = ctx.enter_context(nc.Block())

        @block.sync
        def _(sp):
            for t, s in loads:
                sp.dma_start(t, d["L1_attn_" + s]).then_inc(loaded, 16)
            sp.dma_start(masks[:], d["c_masks"]).then_inc(loaded, 16)
            sp.wait_ge(loaded, LOADED)

        @block.tensor
        def _(pe):
            pe.wait_ge(loaded, LOADED)
            mm, tr = nc.tensor.matmul, nc.tensor.transpose
            with pe.Fori(0, ROUNDS) as i:
                nth = lambda u: i * U + u + 1
                of = lambda u, per, j: i * (U * per) + u * per + j
                for u in range(U):
                    pe.wait_ge(x_added, nth(u))
                    mm(bank[u][0][:], center[:], x[:, bass.ds(i * (U * N) + u * N, N)], start=True,
                       stop=True).then_inc(centered_ready, 1)
                for u in range(U):
                    pe.wait_ge(square_ready, nth(u))
                    mm(bank[u][1][:], mean[:], square[:, u, :], start=True, stop=True).then_inc(var_ready, 1)
                for u in range(U):
                    pe.wait_ge(z0_ready, nth(u))
                    mm(bank[u][2][:], w1[:, 0:P], z_last[:, u, :], start=True, stop=True).then_inc(low_mm, 1)
                    mm(bank[u][3][0:32, :], w1[:, P:P + 32], z_last[:, u, :], start=True, stop=True).then_inc(low4_mm, 1)
                for m in range(4):
                    for u in range(U):
                        pe.wait_ge(low_ready, nth(u))
                        if m == 3:
                            pe.wait_ge(low4_ready, nth(u))
                        mm(bank[u][m][:], w2a[32 * m:32 * m + 32, :], low[32 * m:32 * m + 32, u, :], start=True,
                           stop=True).then_inc(x5_ready, 1)
                for u in range(U):
                    pe.wait_ge(mix_scaled, i * (5 * U) + u + 1)
                    mm(bank[u][0][:], w2b[:], low4[:, u, :], start=True, stop=True).then_inc(x5_ready, 1)
                for j in range(H):
                    for u in range(U):
                        if j == 0:
                            pe.wait_ge(mix_ready, i * (5 * U) + u + 1)
                        pe.wait_ge(mix_scaled, i * (5 * U) + (j + 1) * U + u + 1)
                        mm(bank[u][(j + 1) % 4][:], rW[:, j, :], z(u, 0), start=True, stop=True).then_inc(r_mm, 1)
                for u in range(U):
                    pe.wait_ge(mix_ready, i * (5 * U) + U + u + 1)
                    pe.wait_ge(uq_ready, i * (H * U) + u + 1)
                    mm(bank[u][1][0:LR, :], wA[:], z(u, 1), start=True, stop=True).then_inc(wA_mm, 1)
                for j in range(H):
                    for u in range(U):
                        if j == 0:
                            pe.wait_ge(mix_ready, i * (5 * U) + 2 * U + u + 1)
                        if j < 3:
                            pe.wait_ge(uq_ready, i * (H * U) + (j + 1) * U + u + 1)
                        else:
                            pe.wait_ge(wA_ready, nth(u))
                        mm(bank[u][(j + 2) % 4][:], kW[:, j, :], z(u, 2), start=True, stop=True).then_inc(k_mm, 1)
                for j in range(H):
                    for u in range(U):
                        if j == 0:
                            pe.wait_ge(wA_ready, nth(u))
                        pe.wait_ge(k_ready, i * (H * U) + j * U + u + 1)
                        mm(bank[u][(j + 2) % 4][:], wB[:, j, :], lowrank[:, u, :], start=True, stop=True).then_inc(wB_mm, 1)
                for u in range(U):
                    pe.wait_ge(mix_ready, i * (5 * U) + 3 * U + u + 1)
                    pe.wait_ge(exp_ready, i * (H * U) + u + 1)
                    for t in range(T):
                        last = mm(bank[u][2][:, t * C:(t + 1) * C], z(u, 3)[:, t * C:(t + 1) * C], vW[:], start=True, stop=True)
                    last.then_inc(v_mm, 1)
                for u in range(U):
                    pe.wait_ge(mix_ready, i * (5 * U) + 4 * U + u + 1)
                    pe.wait_ge(exp_ready, i * (H * U) + U + u + 1)
                    mm(bank[u][3][0:LR, :], gA[:], z(u, 4), start=True, stop=True).then_inc(gA_mm, 1)
                for u in range(U):
                    pe.wait_ge(gA_ready, nth(u))
                    pe.wait_ge(exp_ready, i * (H * U) + 2 * U + u + 1)
                    mm(bank[u][0][:], gB[:], lowrank[:, u, :], start=True, stop=True).then_inc(gB_mm, 1)
                for t in range(T):
                    for u in range(U):
                        if t == 0:
                            pe.wait_ge(exp_ready, i * (H * U) + 3 * U + u + 1)
                        elif t == 1:
                            pe.wait_ge(v_ready, nth(u))
                        elif t == 3:
                            pe.wait_ge(g_ready, nth(u))
                        for j in range(H):
                            last = mm(bank[u][(t + 1) % 4][:, j * C:(j + 1) * C], k[:, u, t, j, :], uq[:, u, t, j, :],
                                      start=True, stop=True)
                        last.then_inc(diag_mm, 1)
                for l, h in enumerate(LEVELS):
                    for u in range(U):
                        if l:
                            pe.wait_ge(k_scaled, i * (NL * U) + (l - 1) * U + u + 1)
                            pe.wait_ge(q_scaled, i * (NL * U) + (l - 1) * U + u + 1)
                        for p in range(2):
                            b = (2 * (l % 2) + p + 1) % 4
                            if l < 2:
                                pe.wait_ge(diag_ready, i * (T * U) + (2 * l + p) * U + u + 1)
                            else:
                                pe.wait_ge(merged, i * (2 * NL * U) + (l - 2) * 2 * U + 2 * u + p + 1)
                            for c in range(2 * H):
                                t, j = 2 * p + c // H, c % H
                                last = mm(bank[u][b][:, c * 64:(c + 1) * 64].rearrange("p (n h) -> p n h", h=h),
                                          k[:, u, t, j, :],
                                          q[:, u, t, j, :].rearrange("p (n two h) -> p n two h", two=2, h=h)[:, :, 1, :],
                                          start=True, stop=True)
                            last.then_inc(level_mm, 1)
                for t in range(T - 1):
                    for u in range(U):
                        if t == 0:
                            pe.wait_ge(k_scaled, i * (NL * U) + (NL - 1) * U + u + 1)
                            pe.wait_ge(merged, i * (2 * NL * U) + (NL - 1) * 2 * U + 2 * u + 2)
                        for j in range(H):
                            last = tr(bank[u][t + 1][:, j * C:(j + 1) * C], k[:, u, t, j, :], eye[:])
                        last.then_inc(turned, 1)
                for t in range(T - 1):
                    for u in range(U):
                        pe.wait_ge(kT_ready, i * ((T - 1) * U) + t * U + u + 1)
                        for j in range(H):
                            last = mm(bank[u][0][:, t * P + j * DV:t * P + (j + 1) * DV], kT[:, u, t, j, :],
                                      v[:, u, t, j * DV:(j + 1) * DV], start=True, stop=True)
                        last.then_inc(kv_mm, 1)
                for t in range(T):
                    for u in range(U):
                        if t == 0:
                            pe.wait_ge(q_scaled, i * (NL * U) + (NL - 1) * U + u + 1)
                        else:
                            pe.wait_ge(state_step, i * (5 * U) + [1, 3, 5][t - 1] + u * 5)
                        for j in range(H):
                            out = bank[u][1][j * DV:(j + 1) * DV, t * C:(t + 1) * C]
                            last = mm(out, v[:, u, t, j * DV:(j + 1) * DV], S[:, u, t, j, :], start=True, stop=(t == 0))
                            if t:
                                last = mm(out, state[:, u, t - 1, j, :], q[:, u, t, j, :], start=False, stop=True)
                        if t == T - 1:
                            last.then_inc(o_mm, 1)
                for u in range(U):
                    pe.wait_ge(o_ready, nth(u))
                    mm(bank[u][2][:], center[:], o[:, u, :], start=True, stop=True).then_inc(oc_mm, 1)
                for u in range(U):
                    pe.wait_ge(osquare_ready, nth(u))
                    mm(bank[u][3][:], mean[:], square[:, u, :], start=True, stop=True).then_inc(ovar_mm, 1)
                for u in range(U):
                    pe.wait_ge(o_step, i * (3 * U) + 2 * U + u + 1)
                    mm(bank[u][0][:], oW[:], o[:, u, :], start=True, stop=True).then_inc(out_mm, 1)

        @block.scalar
        def _(act):
            A = nc.scalar.activation
            act.wait_ge(loaded, LOADED)
            act.wait_ge(prepared, 1)
            with act.Fori(0, ROUNDS) as i:
                nth = lambda u: i * U + u + 1

                def by_token(t, u, j):
                    return t[:, u, :, j, :]

                chunks = lambda b: b.rearrange("p (t c) -> p t c", c=C)
                for u in range(U):
                    act.wait_ge(centered_ready, nth(u))
                    A(square[:, u, :], bank[u][0][:], ACT.Square).then_inc(square_ready, 1)
                for u in range(U):
                    act.wait_ge(var_ready, nth(u))
                    A(logvar[:, u, :], bank[u][1][:], ACT.Ln, bias=eps[:, 0:1]).then_inc(log_ready, 1)
                for u in range(U):
                    act.wait_ge(log_ready, nth(u))
                    A(rstd[:, u, :], logvar[:, u, :], ACT.Exp, scale=-0.5).then_inc(rstd_ready, 1)
                for u in range(U):
                    act.wait_ge(low_mm, nth(u))
                    A(low[:, u, :], bank[u][2][:], ACT.Tanh).then_inc(low_ready, 1)
                    act.wait_ge(low4_mm, nth(u))
                    A(low4[:, u, :], bank[u][3][0:32, :], ACT.Tanh).then_inc(low4_ready, 1)
                for j in range(H):
                    for u in range(U):
                        act.wait_ge(r_mm, i * (H * U) + j * U + u + 1)
                        A(by_token(q, u, j), chunks(bank[u][(j + 1) % 4][:]), ACT.Copy).then_inc(q_ready, 1)
                        A(by_token(uq, u, j), chunks(bank[u][(j + 1) % 4][:]), ACT.Copy,
                          scale=bonus[:, j:j + 1]).then_inc(uq_ready, 1)
                for u in range(U):
                    act.wait_ge(wA_mm, nth(u))
                    A(lowrank[:, u, :], bank[u][1][0:LR, :], ACT.Tanh).then_inc(wA_ready, 1)
                for j in range(H):
                    for u in range(U):
                        act.wait_ge(k_mm, i * (H * U) + j * U + u + 1)
                        A(by_token(k, u, j), chunks(bank[u][(j + 2) % 4][:]), ACT.Copy).then_inc(k_ready, 1)
                for j in range(H):
                    for u in range(U):
                        act.wait_ge(wB_mm, i * (H * U) + j * U + u + 1)
                        A(by_token(decay, u, j), chunks(bank[u][(j + 2) % 4][:]), ACT.Exp,
                          bias=w_b[:, j:j + 1]).then_inc(exp_ready, 1)
                for j in range(H):
                    for u in range(U):
                        act.wait_ge(exp_ready, i * (H * U) + j * U + u + 1)
                        A(by_token(decay, u, j), by_token(decay, u, j), ACT.Exp, scale=-1.0).then_inc(decay_ready, 1)
                for u in range(U):
                    act.wait_ge(v_mm, nth(u))
                    A(v[:, u, :, :], chunks(bank[u][2][:]), ACT.Copy).then_inc(v_ready, 1)
                for u in range(U):
                    act.wait_ge(gA_mm, nth(u))
                    A(lowrank[:, u, :], bank[u][3][0:LR, :], ACT.Tanh).then_inc(gA_ready, 1)
                for u in range(U):
                    act.wait_ge(gB_mm, nth(u))
                    A(silu_g[:, u, :], bank[u][0][:], ACT.Tanh, bias=half_gb[:, 0:1], scale=0.5)
                    A(g[:, u, :], bank[u][0][:], ACT.Identity, bias=g_b).then_inc(g_ready, 1)
                for t in range(T - 1):
                    for u in range(U):
                        act.wait_ge(turned, i * ((T - 1) * U) + t * U + u + 1)
                        A(kT[:, u, t, :, :].rearrange("p h c -> p (h c)"), bank[u][t + 1][:], ACT.Copy).then_inc(kT_ready, 1)
                for u in range(U):
                    act.wait_ge(o_mm, nth(u))
                    A(o[:, u, :], bank[u][1][:], ACT.Copy).then_inc(o_ready, 1)
                for u in range(U):
                    act.wait_ge(oc_mm, nth(u))
                    A(square[:, u, :], bank[u][2][:], ACT.Square).then_inc(osquare_ready, 1)
                for u in range(U):
                    act.wait_ge(ovar_mm, nth(u))
                    A(logvar[:, u, :], bank[u][3][:], ACT.Ln, bias=eps[:, 0:1]).then_inc(olog_ready, 1)
                for u in range(U):
                    act.wait_ge(olog_ready, nth(u))
                    A(rstd[:, u, :], logvar[:, u, :], ACT.Exp, scale=-0.5).then_inc(orstd_ready, 1)

        @block.vector
        def _(dve):
            TT, TS, STT = nc.vector.tensor_tensor, nc.vector.tensor_scalar, nc.vector.scalar_tensor_tensor
            dve.wait_ge(loaded, LOADED)
            TS(half_gb[:], g_b, 0.5, None, ALU.mult).then_inc(prepared, 1)
            dve.sem_inc(x_added, U)
            with dve.Fori(0, ROUNDS) as i:
                nth = lambda u: i * U + u + 1
                for u in range(U):
                    dve.wait_ge(rstd_ready, nth(u))
                    TT(xn[:, u, :], bank[u][0][:], rstd[:, u, :], ALU.mult).then_inc(xn_ready, 1)
                for u in range(U):
                    dve.wait_ge(xn_ready, nth(u))
                    TT(delta[:, u, 1:N], xn[:, u, 0:N - 1], xn[:, u, 1:N], ALU.subtract).then_inc(delta_ready, 1)
                    TS(delta[:, u, 0:1], xn[:, u, 0:1], -1.0, None, ALU.mult).then_inc(delta_ready, 1)
                for u in range(U):
                    dve.wait_ge(delta_ready, i * (2 * U) + 2 * u + 2)
                    STT(z_last[:, u, :], delta[:, u, :], mu, xn[:, u, :], ALU.mult, ALU.add).then_inc(z0_ready, 1)
                for m in range(MIX):
                    for u in range(U):
                        dve.wait_ge(x5_ready, i * (5 * U) + m * U + u + 1)
                        if m:
                            dve.wait_ge(mix_ready, i * (5 * U) + (m - 1) * U + u + 1)
                        STT(scaled[:, u, :], bank[u][m % 4][:], x_bias[:, m:m + 1], delta[:, u, :], ALU.add,
                            ALU.mult).then_inc(mix_scaled, 1)
                    for u in range(U):
                        dve.wait_ge(mix_scaled, i * (5 * U) + m * U + u + 1)
                        TT(z(u, m), scaled[:, u, :], xn[:, u, :], ALU.add).then_inc(mix_ready, 1)
                for u in range(U):
                    dve.wait_ge(g_ready, nth(u))
                    STT(silu_g[:, u, :], silu_g[:, u, :], 1.0, g[:, u, :], ALU.add, ALU.mult).then_inc(silu_ready, 1)
                for t in range(T):
                    for u in range(U):
                        dve.wait_ge(diag_mm, i * (T * U) + t * U + u + 1)
                        TT(S[:, u, t, :, :], bank[u][(t + 1) % 4][:].rearrange("p (h c) -> p h c", c=C),
                           broadcast(eye[:], 1, H), ALU.mult).then_inc(diag_ready, 1)
                for l, h in enumerate(LEVELS):
                    for u in range(U):
                        dve.wait_ge(level_mm, i * (2 * NL * U) + 2 * U * l + 2 * u + 2)
                        if l:
                            dve.wait_ge(total_ready, i * ((NL - 1 + 1) * U) + (l - 1) * U + u + 1)
                        else:
                            dve.wait_ge(decay_ready, i * (H * U) + 3 * U + u + 1)
                            dve.wait_ge(diag_ready, i * (T * U) + 3 * U + u + 1)
                        total = halves(decay, u, h)[:, :, :, 0]
                        qh, kh = halves(q, u, h)[:, :, 1, :], halves(k, u, h)[:, :, 0, :]
                        TT(kh, kh, broadcast(total[:, :, 1], 2, h), ALU.mult).then_inc(k_scaled, 1)
                        TT(qh, qh, broadcast(total[:, :, 0], 2, h), ALU.mult).then_inc(q_scaled, 1)
                    for u in range(U):
                        total = halves(decay, u, h)[:, :, :, 0]
                        dve.wait_ge(q_scaled, i * (NL * U) + l * U + u + 1)
                        TT(total[:, :, 0], total[:, :, 0], total[:, :, 1], ALU.mult).then_inc(total_ready, 1)
                    for u in range(U):
                        for p in range(2):
                            b = (2 * (l % 2) + p + 1) % 4
                            Sp = S[:, u, 2 * p:2 * p + 2, :, :].rearrange("p t h c -> p (t h c)") \
                                .rearrange("p (g n two h) -> p g n two h", g=2 * H, two=2, h=h)[:, :, :, 1, :]
                            mask = masks[:, l, :].rearrange("p (n two h) -> p n two h", two=2, h=h)[:, :, 1, :]
                            nc.vector.copy_predicated(
                                Sp, broadcast(mask, 1, 2 * H),
                                bank[u][b][:].rearrange("p (g n h) -> p g n h", g=2 * H, h=h)).then_inc(merged, 1)
                for u in range(U):
                    kv = lambda t: bank[u][0][:, t * P:(t + 1) * P].rearrange("p (h v) -> p h v", v=DV)
                    dve.wait_ge(kv_mm, i * ((T - 1) * U) + (T - 2) * U + u + 1)
                    nc.vector.tensor_copy(state[:, u, 0, :, :], kv(0)).then_inc(state_step, 1)
                    for t in range(1, T - 1):
                        dve.wait_ge(state_step, i * (5 * U) + 5 * u + 2 * t - 1)
                        if t == 1:
                            dve.wait_ge(total_ready, i * (NL * U) + (NL - 1) * U + u + 1)
                        TT(state[:, u, t, :, :], state[:, u, t - 1, :, :],
                           broadcast(decay[:, u, t, :, 0], 2, DV), ALU.mult).then_inc(state_step, 1)
                        dve.wait_ge(state_step, i * (5 * U) + 5 * u + 2 * t)
                        TT(state[:, u, t, :, :], kv(t), state[:, u, t, :, :], ALU.add).then_inc(state_step, 1)
                for u in range(U):
                    dve.wait_ge(orstd_ready, nth(u))
                    TT(o[:, u, :], bank[u][2][:], rstd[:, u, :], ALU.mult).then_inc(o_step, 1)
                for u in range(U):
                    dve.wait_ge(o_step, i * (3 * U) + u + 1)
                    TS(o[:, u, :], o[:, u, :], gn_w, gn_b, ALU.mult, ALU.add).then_inc(o_step, 1)
                for u in range(U):
                    dve.wait_ge(o_step, i * (3 * U) + U + u + 1)
                    dve.wait_ge(silu_ready, nth(u))
                    STT(o[:, u, :], o[:, u, :], 0.5, silu_g[:, u, :], ALU.mult, ALU.mult).then_inc(o_step, 1)
                for u in range(U):
                    dve.wait_ge(out_mm, nth(u))
                    xs = x[:, bass.ds(i * (U * N) + u * N, N)]
                    TT(xs, bank[u][0][:], xs, ALU.add).then_inc(x_added, 1)



def fp4_ffn_phase(nc, d, x, xn, eye):
    U = 2
    NX = N // QB
    NH = SUB * I // QB
    IC = [P, P, I - 2 * P]
    NW = (6 * P + I) // QB
    QSTEPS = 9
    with ExitStack() as ctx:
        sem = lambda s: ctx.enter_context(nc.semaphore(f"ffn_{s}"))
        sb = lambda s, shape, dt=F32: ctx.enter_context(nc.sbuf_tensor(f"ffn_{s}", shape, dt))
        bank = [[ctx.enter_context(nc.psum_tensor(f"ffn_bank{u}{b}", [P, N], F32)) for b in range(4)] for u in range(U)]
        w_raw = sb("w_raw", [P, NW, QB])
        w_in = sb("w_in", [P, 2, I])
        w_down = sb("w_down", [P, 3, P])
        xt, xT = sb("xt", [P, U, N]), sb("xT", [P, U, NX, QB])
        xq = sb("xq", [P, U, N])
        silu = sb("silu", [P, U, 2, I])
        h = sb("h", [P, U, NH, QB])
        hq = sb("hq", [P, U, 3, N])
        amax, scale, inv = (sb(s, [P, U, NH]) for s in ("amax", "scale", "inv"))
        v, a = sb("v", [P, U, NH, QB]), sb("a", [P, U, NH, QB])
        low, c = sb("low", [P, U, NH, QB]), sb("c", [P, U, NH, QB])
        loaded, zeroed, qstep = sem("loaded"), sem("zeroed"), sem("qstep")
        scaled, magnitude, signed, quantised = sem("scaled"), sem("magnitude"), sem("signed"), sem("quantised")
        w_turned, w_placed = sem("w_turned"), sem("w_placed")
        xt_ready, x_turned, xT_ready, xq_turned, xq_ready = sem("xt"), sem("x_turned"), sem("xT"), sem("xq_turned"), sem("xq")
        gate_up, silu_ready, h_ready, h_turned, hq_ready = sem("gate_up"), sem("silu"), sem("h"), sem("h_turned"), sem("hq")
        down_ready, x_added = sem("down"), sem("x_added")
        ROUNDS = SEQS // U
        mask_sign = -2147483648

        def q_vector(dve, src, u, nb, k, dst):
            amx, scl, inb = amax[:, u, 0:nb], scale[:, u, 0:nb], inv[:, u, 0:nb]
            vv, aa, cc, ll = v[:, u, 0:nb, :], a[:, u, 0:nb, :], c[:, u, 0:nb, :], low[:, u, 0:nb, :]
            base = k * QSTEPS
            nc.vector.tensor_reduce(amx, src, AX.X, ALU.max, apply_absolute_value=True).then_inc(qstep, 1)
            dve.wait_ge(qstep, base + 1)
            nc.vector.tensor_scalar(scl, amx, 1.0 / 6.0, 1e-12, ALU.mult, ALU.max).then_inc(qstep, 1)
            dve.wait_ge(qstep, base + 2)
            nc.vector.reciprocal(inb, scl).then_inc(qstep, 1)
            dve.wait_ge(qstep, base + 3)
            nc.vector.tensor_tensor(vv, src, broadcast(inb, 2, QB), ALU.mult).then_inc(scaled, 1)
            dve.wait_ge(magnitude, k + 1)
            nc.vector.tensor_scalar(ll, aa, 1.0, MAGIC, ALU.min, ALU.add).then_inc(qstep, 1)
            nc.vector.tensor_scalar(cc, aa, 1.0, SPLIT, ALU.max, ALU.mult).then_inc(qstep, 1)
            dve.wait_ge(qstep, base + 4)
            nc.vector.tensor_scalar(ll, ll, -MAGIC, -1.0, ALU.add, ALU.add).then_inc(qstep, 1)
            dve.wait_ge(qstep, base + 5)
            nc.vector.scalar_tensor_tensor(aa, aa, 1.0, cc, ALU.max, ALU.subtract).then_inc(qstep, 1)
            dve.wait_ge(qstep, base + 7)
            nc.vector.tensor_tensor(cc, cc, aa, ALU.add).then_inc(qstep, 1)
            dve.wait_ge(qstep, base + 8)
            nc.vector.tensor_tensor(cc, cc, ll, ALU.add).then_inc(qstep, 1)
            dve.wait_ge(qstep, base + 9)
            nc.vector.scalar_tensor_tensor(cc.bitcast(I32), vv.bitcast(I32), mask_sign, cc.bitcast(I32),
                                           ALU.bitwise_and, ALU.bitwise_or).then_inc(signed, 1)
            dve.wait_ge(signed, k + 1)
            nc.vector.tensor_tensor(dst, cc, broadcast(scl, 2, QB), ALU.mult).then_inc(quantised, 1)

        def q_scalar(act, u, nb, k):
            act.wait_ge(scaled, k + 1)
            nc.scalar.activation(a[:, u, 0:nb, :], v[:, u, 0:nb, :], ACT.Abs, scale=NUDGE).then_inc(magnitude, 1)

        block = ctx.enter_context(nc.Block())

        @block.sync
        def _(sp):
            sp.wait_ge(zeroed, 1)
            wr = w_raw[:].rearrange("p b q -> p (b q)")
            for m, s in enumerate(["w_gate", "w_up"]):
                for r, rows in enumerate(IC):
                    sp.dma_start(wr[0:rows, (3 * m + r) * P:(3 * m + r + 1) * P],
                                 d["L1_ffn_" + s][r * P:r * P + rows, :]).then_inc(loaded, 16)
            sp.dma_start(wr[:, 6 * P:6 * P + I], d["L1_ffn_w_down"]).then_inc(loaded, 16)
            sp.wait_ge(loaded, 7 * 16)

        @block.gpsimd
        def _(pool):
            nc.gpsimd.memset(w_raw[:], 0.0).then_inc(zeroed, 1)

        @block.vector
        def _(dve):
            dve.wait_ge(loaded, 7 * 16)
            q_vector(dve, w_raw[:], 0, NW, 0, w_raw[:])
            for m in range(2):
                dve.wait_ge(w_turned, m + 1)
                nc.vector.tensor_copy(w_in[:, m, :], bank[0][m][:, 0:I]).then_inc(w_placed, 1)
            dve.wait_ge(w_turned, 3)
            for r, rows in enumerate(IC):
                nc.vector.tensor_copy(w_down[0:rows, r, :], bank[0][2][0:rows, r * P:(r + 1) * P]).then_inc(w_placed, 1)
            with dve.Fori(0, ROUNDS) as i:
                for u in range(U):
                    n = i * U + u + 1
                    dve.wait_ge(xT_ready, n)
                    q_vector(dve, xT[:, u, :, :], u, NX, i * (2 * U) + u + 1, xT[:, u, :, :])
                for t in range(SUB):
                    for u in range(U):
                        dve.wait_ge(silu_ready, i * (U * SUB) + t * U + u + 1)
                        hrow = h[:, u, t * (I // QB):(t + 1) * (I // QB), :].rearrange("p b q -> p (b q)")
                        nc.vector.tensor_tensor(hrow, bank[u][2 * (t % 2) + 1][:, 0:I], silu[:, u, t % 2, :],
                                                ALU.mult).then_inc(h_ready, 1)
                for u in range(U):
                    dve.wait_ge(h_ready, i * (U * SUB) + (SUB - 1) * U + u + 1)
                    q_vector(dve, h[:, u, :, :], u, NH, i * (2 * U) + U + u + 1, h[:, u, :, :])
                for u in range(U):
                    dve.wait_ge(down_ready, i * U + u + 1)
                    xs = x[:, bass.ds(i * (U * N) + u * N, N)]
                    nc.vector.tensor_tensor(xs, bank[u][3][:], xs, ALU.add).then_inc(x_added, 1)

        @block.scalar
        def _(act):
            q_scalar(act, 0, NW, 0)
            with act.Fori(0, ROUNDS) as i:
                for u in range(U):
                    nc.scalar.activation(xt[:, u, :], xn[:, bass.ds(i * (U * N) + u * N, N)], ACT.Copy).then_inc(xt_ready, 1)
                for u in range(U):
                    act.wait_ge(x_turned, i * U + u + 1)
                    nc.scalar.activation(xT[:, u, :, :].rearrange("p b q -> p (b q)"), bank[u][0][:],
                                         ACT.Copy).then_inc(xT_ready, 1)
                for u in range(U):
                    q_scalar(act, u, NX, i * (2 * U) + u + 1)
                for u in range(U):
                    act.wait_ge(xq_turned, i * U + u + 1)
                    nc.scalar.activation(xq[:, u, :], bank[u][1][:], ACT.Copy).then_inc(xq_ready, 1)
                for t in range(SUB):
                    for u in range(U):
                        act.wait_ge(gate_up, i * (U * SUB) + t * U + u + 1)
                        if t >= 2:
                            act.wait_ge(h_ready, i * (U * SUB) + (t - 2) * U + u + 1)
                        nc.scalar.activation(silu[:, u, t % 2, :], bank[u][2 * (t % 2)][:, 0:I], ACT.Silu).then_inc(silu_ready, 1)
                for u in range(U):
                    q_scalar(act, u, NH, i * (2 * U) + U + u + 1)
                for u in range(U):
                    act.wait_ge(h_turned, i * U + u + 1)
                    for r, rows in enumerate(IC):
                        nc.scalar.activation(hq[0:rows, u, r, :], bank[u][r][0:rows, :], ACT.Copy).then_inc(hq_ready, 1)

        @block.tensor
        def _(pe):
            pe.wait_ge(quantised, 1)
            wr = w_raw[:].rearrange("p b q -> p (b q)")
            for m in range(2):
                for r, rows in enumerate(IC):
                    last = nc.tensor.transpose(bank[0][m][:, r * P:r * P + rows],
                                               wr[0:rows, (3 * m + r) * P:(3 * m + r + 1) * P], eye[0:rows, 0:rows])
                last.then_inc(w_turned, 1)
            for r, rows in enumerate(IC):
                last = nc.tensor.transpose(bank[0][2][0:rows, r * P:(r + 1) * P],
                                           wr[:, 6 * P + r * P:6 * P + r * P + rows], eye[:])
            last.then_inc(w_turned, 1)
            pe.wait_ge(w_placed, 5)
            with pe.Fori(0, ROUNDS) as i:
                for u in range(U):
                    pe.wait_ge(xt_ready, i * U + u + 1)
                    for t in range(SUB):
                        last = nc.tensor.transpose(bank[u][0][:, t * P:(t + 1) * P], xt[:, u, t * P:(t + 1) * P], eye[:])
                    last.then_inc(x_turned, 1)
                for u in range(U):
                    pe.wait_ge(quantised, i * (2 * U) + u + 2)
                    xTu = xT[:, u, :, :].rearrange("p b q -> p (b q)")
                    for t in range(SUB):
                        last = nc.tensor.transpose(bank[u][1][:, t * P:(t + 1) * P], xTu[:, t * P:(t + 1) * P], eye[:])
                    last.then_inc(xq_turned, 1)
                for t in range(SUB):
                    for u in range(U):
                        pe.wait_ge(xq_ready, i * U + u + 1)
                        if t >= 2:
                            pe.wait_ge(h_ready, i * (U * SUB) + (t - 2) * U + u + 1)
                        b = 2 * (t % 2)
                        for m in range(2):
                            last = nc.tensor.matmul(bank[u][b + m][:, 0:I], xq[:, u, t * P:(t + 1) * P], w_in[:, m, :],
                                                    start=True, stop=True)
                        last.then_inc(gate_up, 1)
                for u in range(U):
                    pe.wait_ge(quantised, i * (2 * U) + U + u + 2)
                    hu = h[:, u, :, :].rearrange("p b q -> p (b q)")
                    for r, rows in enumerate(IC):
                        for t in range(SUB):
                            last = nc.tensor.transpose(bank[u][r][0:rows, t * P:(t + 1) * P],
                                                       hu[:, t * I + r * P:t * I + r * P + rows], eye[:])
                    last.then_inc(h_turned, 1)
                for u in range(U):
                    pe.wait_ge(hq_ready, i * (3 * U) + 3 * u + 3)
                    for r, rows in enumerate(IC):
                        last = nc.tensor.matmul(bank[u][3][:], w_down[0:rows, r, :], hq[0:rows, u, r, :],
                                                start=(r == 0), stop=(r == 2))
                    last.then_inc(down_ready, 1)



def host_layout(inputs):
    a = {k: np.asarray(v) for k, v in inputs.items()}
    t = {"x": a["L0_attn_x"].reshape(TOK, P).T}
    for s in ("Wg_w", "Wr_w", "Wk_w", "Wv_w", "Wo_w"):
        t["L0_attn_" + s] = a["L0_attn_" + s].T
    for s in ("Wg_b", "Wr_b", "Wk_b", "Wv_b", "Wo_b", "mg", "mr", "mk", "mv", "w", "u"):
        t["L0_attn_" + s] = a["L0_attn_" + s].reshape(P, 1)
    t["L0_ffn_gate_w"] = a["L0_ffn_gate_w"].T
    t["L0_ffn_w1"] = a["L0_ffn_w1"].transpose(2, 0, 1)
    t["L0_ffn_w3"] = a["L0_ffn_w3"].transpose(2, 0, 1)
    t["L0_ffn_w2"] = a["L0_ffn_w2"].reshape(E, P, FC, P).transpose(3, 0, 2, 1)
    for s in ("w_gate", "w_up", "w_down"):
        t["L1_ffn_" + s] = a["L1_ffn_" + s]
    L = lambda s: a["L1_attn_" + s]
    for s in ("xp_W1", "v_W", "o_W", "w_A", "g_A", "g_B", "x_bias", "bonus"):
        t["L1_attn_" + s] = L(s).T
    t["L1_attn_xp_W2a"], t["L1_attn_xp_W2b"] = L("xp_W2").T[:P], L("xp_W2").T[P:]
    for s in ("r_W", "k_W"):
        t["L1_attn_" + s] = L(s).T.reshape(P, H, DK)
    t["L1_attn_w_B"] = L("w_B").T.reshape(LR, H, DK)
    t["L1_attn_w_b"] = L("w_b").reshape(H, DK).T
    for s in ("xp_mu", "g_b", "gn_w", "gn_b"):
        t["L1_attn_" + s] = L(s).reshape(P, 1)
    return t


def kernel(**inputs):
    import concourse.bacc as bacc
    from concourse.bass_utils import run_bass_kernel_spmd as run

    nc = bacc.Bacc("TRN2", target_bir_lowering=False, num_devices=1)
    arrays, d = {}, {}
    for name, a in {**host_layout(inputs), **constants()}.items():
        a = np.ascontiguousarray(a)
        arrays[f"in_{name}"] = a
        d[name] = nc.dram_tensor(f"in_{name}", a.shape, mybir.dt.from_np(a.dtype), kind="ExternalInput").ap()
    out = nc.dram_tensor("out_x", (P, TOK), F32, kind="ExternalOutput").ap()
    build(nc, d, out)
    r = run(nc, [arrays], core_ids=[0])
    return np.ascontiguousarray(r.results[0]["out_x"].T).reshape(SEQS, SEQ, P)
```

```python
from contextlib import ExitStack

import numpy as np

import concourse.bass as bass
from concourse import mybir

F32R = mybir.dt.float32r
F32 = mybir.dt.float32
I32 = mybir.dt.int32
ALU = mybir.AluOpType
ACT = mybir.ActivationFunctionType
AX = mybir.AxisListType

P = 128
SEQS, SEQ = 16, 512
TOK = SEQS * SEQ
N = 512
EPS = 1e-5

E, F = 8, 512
FC = F // P
SUB = N // P
H, DK, DV = 4, 128, 32
C = 128
LEVELS = [1, 2, 4, 8, 16, 32, 64]
MIX, LR = 5, 64
I = 352
QB = 16
BIG = -3.0e38
MAGIC = 1.5 * 2.0 ** 22
SPLIT = 2.0 ** 22 + 1.0
NUDGE = 1.0 - 2.0 ** -24


def constants():
    eye = np.eye(P, dtype=np.float32)
    mean = np.full((P, P), 1.0 / P, np.float32)
    group = np.kron(np.eye(16), np.full((8, 8), 1.0 / 8)).astype(np.float32)
    j, i = np.arange(C)[:, None], np.arange(C)[None, :]
    masks = [((i // h) % 2 == 1) & (i // (2 * h) == j // (2 * h)) & ((j // h) % 2 == 0) for h in LEVELS]
    masks = np.stack(masks, 1).astype(np.int32)
    first = np.broadcast_to(np.arange(E, 0, -1, dtype=np.float32), (P, E))
    return {"c_eye": eye, "c_mean": mean, "c_center": eye - mean, "c_group": group,
            "c_gcenter": eye - group, "c_masks": masks, "c_first": np.ascontiguousarray(first),
            "c_pick": np.tile(np.eye(E, dtype=np.float32), (2, 1))}


def broadcast(ap, axis, count):
    v = ap.unsqueeze(axis)
    shape = list(v.shape)
    shape[axis] = count
    return v.broadcast_to(shape)


def layernorm_phase(nc, name, x, xn, c_center, c_mean, eps, sems, done):
    U = 4
    tiles, norms = done * (TOK // N), done * (TOK // N + U)
    with ExitStack() as ctx:
        sb = lambda s, shape: ctx.enter_context(nc.sbuf_tensor(f"{name}_{s}", shape, F32))
        centered = [ctx.enter_context(nc.psum_tensor(f"{name}_centered{u}", [P, N], F32)) for u in range(U)]
        var = [ctx.enter_context(nc.psum_tensor(f"{name}_var{u}", [P, N], F32)) for u in range(U)]
        square = sb("square", [P, U, N])
        logvar = sb("logvar", [P, U, N])
        rstd = sb("rstd", [P, U, N])
        centered_ready, square_ready, var_ready, log_ready, rstd_ready, normed = sems
        block = ctx.enter_context(nc.Block())

        @block.tensor
        def _(pe):
            with pe.Fori(0, TOK // (U * N)) as i:
                for u in range(U):
                    pe.wait_ge(normed, i * U + (norms + u + 1))
                    nc.tensor.matmul(centered[u][:], c_center[:], x[:, bass.ds(i * (U * N) + u * N, N)],
                                     start=True, stop=True).then_inc(centered_ready, 1)
                for u in range(U):
                    pe.wait_ge(square_ready, i * U + (tiles + u + 1))
                    nc.tensor.matmul(var[u][:], c_mean[:], square[:, u, :], start=True, stop=True).then_inc(var_ready, 1)

        @block.scalar
        def _(act):
            with act.Fori(0, TOK // (U * N)) as i:
                for u in range(U):
                    act.wait_ge(centered_ready, i * U + (tiles + u + 1))
                    nc.scalar.activation(square[:, u, :], centered[u][:], ACT.Square).then_inc(square_ready, 1)
                for u in range(U):
                    act.wait_ge(var_ready, i * U + (tiles + u + 1))
                    nc.scalar.activation(logvar[:, u, :], var[u][:], ACT.Ln, bias=eps[:, 0:1]).then_inc(log_ready, 1)
                for u in range(U):
                    act.wait_ge(log_ready, i * U + (tiles + u + 1))
                    act.wait_ge(normed, i * U + (norms + u + 1))
                    nc.scalar.activation(rstd[:, u, :], logvar[:, u, :], ACT.Exp, scale=-0.5).then_inc(rstd_ready, 1)

        @block.vector
        def _(dve):
            dve.sem_inc(normed, U)
            with dve.Fori(0, TOK // (U * N)) as i:
                for u in range(U):
                    dve.wait_ge(rstd_ready, i * U + (tiles + u + 1))
                    nc.vector.tensor_tensor(xn[:, bass.ds(i * (U * N) + u * N, N)], centered[u][:], rstd[:, u, :],
                                            ALU.mult).then_inc(normed, 1)


def build(nc, d, out):
    with ExitStack() as ctx:
        sb = lambda s, shape, dt=F32: ctx.enter_context(nc.sbuf_tensor(s, shape, dt))
        x = sb("x", [P, TOK])
        eye, mean, center = sb("eye", [P, P]), sb("mean", [P, P]), sb("center", [P, P])
        group, gcenter = sb("group", [P, P]), sb("gcenter", [P, P])
        eps = sb("eps", [P, 1])
        loaded = ctx.enter_context(nc.semaphore("loaded"))
        eps_set = ctx.enter_context(nc.semaphore("eps_set"))
        norm_sems = [ctx.enter_context(nc.semaphore(f"norm_{s}"))
                     for s in ("centered", "square", "var", "log", "rstd", "normed")]
        pairs = [(eye, "c_eye"), (mean, "c_mean"), (center, "c_center"), (group, "c_group"), (gcenter, "c_gcenter")]
        with nc.Block() as block:
            @block.sync
            def _(sp):
                for t, name in pairs:
                    sp.dma_start(t[:], d[name]).then_inc(loaded, 16)
                for q in range(4):
                    sp.dma_start(x[:, q * TOK // 4:(q + 1) * TOK // 4],
                                 d["x"][:, q * TOK // 4:(q + 1) * TOK // 4]).then_inc(loaded, 16)
                sp.wait_ge(loaded, 16 * (len(pairs) + 4))

            @block.gpsimd
            def _(pool):
                nc.gpsimd.memset(eps[:], EPS).then_inc(eps_set, 1)
                pool.wait_ge(eps_set, 1)
        with nc.sbuf_tensor("xn0", [P, TOK], F32) as xn, nc.sbuf_tensor("wte", [P, TOK // P, E], F32) as wte:
            layernorm_phase(nc, "ln0", x, xn, center, mean, eps, norm_sems, 0)
            mix_attention_phase(nc, d, x, xn, gcenter, group, eps)
            layernorm_phase(nc, "ln1", x, xn, center, mean, eps, norm_sems, 1)
            moe_route_phase(nc, d, xn, wte)
            moe_dense_phase(nc, d, x, xn, wte, eye)
        rwkv_phase(nc, d, x, center, mean, eye, eps)
        with nc.sbuf_tensor("xn1", [P, TOK], F32) as xn:
            layernorm_phase(nc, "ln3", x, xn, center, mean, eps, norm_sems, 2)
            fp4_ffn_phase(nc, d, x, xn, eye)
        stored = ctx.enter_context(nc.semaphore("stored"))
        with nc.Block() as block:
            @block.sync
            def _(sp):
                for q in range(4):
                    sp.dma_start(out[:, q * TOK // 4:(q + 1) * TOK // 4],
                                 x[:, q * TOK // 4:(q + 1) * TOK // 4]).then_inc(stored, 16)
                sp.wait_ge(stored, 64)


def mix_attention_phase(nc, d, x, xn, gcenter, group, eps):
    U = 2
    names = ["k", "v", "g", "r"]
    with ExitStack() as ctx:
        sem = lambda s: ctx.enter_context(nc.semaphore(f"l0a_{s}"))
        sb = lambda s, shape: ctx.enter_context(nc.sbuf_tensor(f"l0a_{s}", shape, F32))
        bank = [[ctx.enter_context(nc.psum_tensor(f"l0a_bank{u}{b}", [P, N], F32)) for b in range(4)] for u in range(U)]
        W = sb("W", [P, 5, P])
        cols = sb("cols", [P, 11])
        mk, mv, mg, mr, bk, bv, bg, br, bo, w, u_ = [cols[:, j:j + 1] for j in range(11)]
        mm1 = sb("mm1", [P, 4])
        hbg = sb("hbg", [P, 1])
        ew, dec = sb("ew", [P, 1]), sb("dec", [P, 1])
        decay = sb("decay", [P, N])
        diff = sb("diff", [P, U, N])
        mix = sb("mix", [P, U, 4, N])
        k, th, kv, wkv, rw = (sb(s, [P, U, N]) for s in ("k", "th", "kv", "wkv", "rw"))
        acc = sb("acc", [P, U, N])
        square, logvar, rstd, gate, o = (sb(s, [P, U, N]) for s in ("square", "logvar", "rstd", "gate", "o"))
        loaded, prepared, ew_ready, dec_ready = sem("loaded"), sem("prepared"), sem("ew"), sem("dec")
        diff_ready, mixed = sem("diff"), sem("mixed")
        projected = {s: sem(f"proj_{s}") for s in names}
        k_ready, th_ready, kv_ready, acc_ready, wkv_ready = sem("k"), sem("th"), sem("kv"), sem("acc"), sem("wkv")
        rw_ready, centered_ready, square_ready, var_ready = sem("rw"), sem("centered"), sem("square"), sem("var")
        log_ready, rstd_ready, gate_ready, o_ready = sem("log"), sem("rstd"), sem("gate"), sem("o")
        out_ready, x_added = sem("out"), sem("x_added")
        vecs = ["L0_attn_mk", "L0_attn_mv", "L0_attn_mg", "L0_attn_mr", "L0_attn_Wk_b", "L0_attn_Wv_b",
                "L0_attn_Wg_b", "L0_attn_Wr_b", "L0_attn_Wo_b", "L0_attn_w", "L0_attn_u"]
        block = ctx.enter_context(nc.Block())
        ROUNDS = SEQS // U

        @block.sync
        def _(sp):
            for j, s in enumerate(["Wk_w", "Wv_w", "Wg_w", "Wr_w", "Wo_w"]):
                sp.dma_start(W[:, j, :], d["L0_attn_" + s]).then_inc(loaded, 16)
            for j, s in enumerate(vecs):
                sp.dma_start(cols[:, j:j + 1], d[s]).then_inc(loaded, 16)
            sp.wait_ge(loaded, 256)

        @block.tensor
        def _(pe):
            pe.wait_ge(loaded, 256)
            with pe.Fori(0, ROUNDS) as i:
                for j, s in enumerate(names):
                    for u in range(U):
                        n = i * U + u + 1
                        pe.wait_ge(mixed, i * (4 * U) + j * U + u + 1)
                        if s == "g":
                            pe.wait_ge(x_added, n)
                        nc.tensor.matmul(bank[u][j][:], W[:, j, :], mix[:, u, j, :], start=True,
                                         stop=True).then_inc(projected[s], 1)
                for u in range(U):
                    n = i * U + u + 1
                    pe.wait_ge(rw_ready, n)
                    pe.wait_ge(k_ready, n)
                    nc.tensor.matmul(bank[u][0][:], gcenter[:], rw[:, u, :], start=True,
                                     stop=True).then_inc(centered_ready, 1)
                for u in range(U):
                    n = i * U + u + 1
                    pe.wait_ge(square_ready, n)
                    nc.tensor.matmul(bank[u][1][:], group[:], square[:, u, :], start=True,
                                     stop=True).then_inc(var_ready, 1)
                for u in range(U):
                    n = i * U + u + 1
                    pe.wait_ge(o_ready, n)
                    nc.tensor.matmul(bank[u][2][:], W[:, 4, :], o[:, u, :], start=True, stop=True).then_inc(out_ready, 1)

        @block.scalar
        def _(act):
            act.wait_ge(loaded, 256)
            act.wait_ge(prepared, 2)
            nc.scalar.activation(ew[:], w, ACT.Exp).then_inc(ew_ready, 1)
            act.wait_ge(ew_ready, 1)
            nc.scalar.activation(dec[:], ew[:], ACT.Exp, scale=-1.0).then_inc(dec_ready, 1)
            with act.Fori(0, ROUNDS) as i:
                for u in range(U):
                    n = i * U + u + 1
                    act.wait_ge(projected["k"], n)
                    nc.scalar.activation(k[:, u, :], bank[u][0][:], ACT.Identity, bias=bk).then_inc(k_ready, 1)
                for u in range(U):
                    n = i * U + u + 1
                    act.wait_ge(projected["g"], n)
                    nc.scalar.activation(th[:, u, :], bank[u][2][:], ACT.Tanh, bias=hbg[:, 0:1],
                                         scale=0.5).then_inc(th_ready, 1)
                for u in range(U):
                    n = i * U + u + 1
                    act.wait_ge(centered_ready, n)
                    nc.scalar.activation(square[:, u, :], bank[u][0][:], ACT.Square).then_inc(square_ready, 1)
                for u in range(U):
                    n = i * U + u + 1
                    act.wait_ge(var_ready, n)
                    nc.scalar.activation(logvar[:, u, :], bank[u][1][:], ACT.Ln, bias=eps[:, 0:1]).then_inc(log_ready, 1)
                for u in range(U):
                    n = i * U + u + 1
                    act.wait_ge(log_ready, n)
                    nc.scalar.activation(rstd[:, u, :], logvar[:, u, :], ACT.Exp, scale=-0.5).then_inc(rstd_ready, 1)

        @block.vector
        def _(dve):
            dve.wait_ge(loaded, 256)
            nc.vector.tensor_scalar(mm1[:], cols[:, 0:4], -1.0, None, ALU.add).then_inc(prepared, 1)
            nc.vector.tensor_scalar(hbg[:], bg, 0.5, None, ALU.mult).then_inc(prepared, 1)
            dve.wait_ge(dec_ready, 1)
            nc.vector.tensor_copy(decay[:], dec[:, 0:1].broadcast_to([P, N])).then_inc(prepared, 1)
            dve.sem_inc(x_added, U)
            dve.wait_ge(prepared, 3)

            def mixes(i):
                for u in range(U):
                    at = i * (U * N) + u * N
                    nc.vector.tensor_tensor(diff[:, u, 1:N], xn[:, bass.ds(at + 1, N - 1)], xn[:, bass.ds(at, N - 1)],
                                            ALU.subtract).then_inc(diff_ready, 1)
                    nc.vector.tensor_tensor(diff[:, u, 0:1], xn[:, bass.ds(at, 1)], xn[:, bass.ds(at + N - 1, 1)],
                                            ALU.subtract).then_inc(diff_ready, 1)
                for j in range(4):
                    for u in range(U):
                        dve.wait_ge(diff_ready, i * (2 * U) + 2 * u + 2)
                        nc.vector.scalar_tensor_tensor(mix[:, u, j, :], diff[:, u, :], mm1[:, j:j + 1],
                                                       xn[:, bass.ds(i * (U * N) + u * N, N)], ALU.mult,
                                                       ALU.add).then_inc(mixed, 1)

            def attend(i):
                for u in range(U):
                    n = i * U + u + 1
                    dve.wait_ge(projected["v"], n)
                    dve.wait_ge(k_ready, n)
                    nc.vector.scalar_tensor_tensor(kv[:, u, :], bank[u][1][:], bv, k[:, u, :], ALU.add,
                                                   ALU.mult).then_inc(kv_ready, 1)
                for u in range(U):
                    n = i * U + u + 1
                    dve.wait_ge(kv_ready, n)
                    nc.vector.tensor_tensor_scan(acc[:, u, :], decay[:], kv[:, u, :], 0.0, ALU.mult,
                                                 ALU.add).then_inc(acc_ready, 1)
                for u in range(U):
                    n = i * U + u + 1
                    dve.wait_ge(acc_ready, n)
                    nc.vector.scalar_tensor_tensor(wkv[:, u, :], kv[:, u, :], u_, acc[:, u, :], ALU.mult,
                                                   ALU.add).then_inc(wkv_ready, 1)
                for u in range(U):
                    n = i * U + u + 1
                    dve.wait_ge(wkv_ready, n)
                    dve.wait_ge(projected["r"], n)
                    nc.vector.scalar_tensor_tensor(rw[:, u, :], bank[u][3][:], br, wkv[:, u, :], ALU.add,
                                                   ALU.mult).then_inc(rw_ready, 1)

            def finish(i):
                for u in range(U):
                    n = i * U + u + 1
                    dve.wait_ge(rstd_ready, n)
                    dve.wait_ge(th_ready, n)
                    nc.vector.scalar_tensor_tensor(gate[:, u, :], th[:, u, :], 1.0, rstd[:, u, :], ALU.add,
                                                   ALU.mult).then_inc(gate_ready, 1)
                for u in range(U):
                    n = i * U + u + 1
                    dve.wait_ge(gate_ready, n)
                    nc.vector.scalar_tensor_tensor(o[:, u, :], bank[u][0][:], 0.5, gate[:, u, :], ALU.mult,
                                                   ALU.mult).then_inc(o_ready, 1)
                for u in range(U):
                    n = i * U + u + 1
                    at = i * (U * N) + u * N
                    dve.wait_ge(out_ready, n)
                    nc.vector.scalar_tensor_tensor(x[:, bass.ds(at, N)], bank[u][2][:], bo, x[:, bass.ds(at, N)],
                                                   ALU.add, ALU.add).then_inc(x_added, 1)

            mixes(0)
            with dve.Fori(0, ROUNDS - 1) as i:
                attend(i)
                mixes(i + 1)
                finish(i)
            attend(ROUNDS - 1)
            finish(ROUNDS - 1)


def moe_route_phase(nc, d, xn, wte):
    G = TOK // P
    with ExitStack() as ctx:
        sem = lambda s: ctx.enter_context(nc.semaphore(f"route_{s}"))
        sb = lambda s, shape: ctx.enter_context(nc.sbuf_tensor(f"route_{s}", shape, F32))
        gate_w, first = sb("gate_w", [P, E]), sb("first", [P, E])
        scores = ctx.enter_context(nc.psum_tensor("route_scores", [P, G, E], F32))
        L, L2, s1, s2, s3, one1, keep = (sb(s, [P, G, E]) for s in ("L", "L2", "s1", "s2", "s3", "one1", "keep"))
        m1, m2, r, t = (sb(s, [P, G]) for s in ("m1", "m2", "r", "t"))
        loaded, scored, step, exped = sem("loaded"), sem("scored"), sem("step"), sem("exped")
        block = ctx.enter_context(nc.Block())
        over = lambda v: broadcast(v[:], 2, E)
        firstb = broadcast(first[:], 1, G)

        @block.sync
        def _(sp):
            sp.dma_start(gate_w[:], d["L0_ffn_gate_w"]).then_inc(loaded, 16)
            sp.dma_start(first[:], d["c_first"]).then_inc(loaded, 16)
            sp.wait_ge(loaded, 32)

        @block.tensor
        def _(pe):
            pe.wait_ge(loaded, 32)
            for g in range(G):
                last = nc.tensor.matmul(scores[:, g, :], xn[:, g * P:(g + 1) * P], gate_w[:], start=True, stop=True)
            last.then_inc(scored, 1)

        @block.scalar
        def _(act):
            act.wait_ge(step, 7)
            nc.scalar.activation(s1[:], s1[:], ACT.Exp).then_inc(exped, 1)
            act.wait_ge(step, 22)
            nc.scalar.activation(s1[:], s1[:], ACT.Exp).then_inc(exped, 1)

        @block.vector
        def _(dve):
            count = [0]

            def then(ins):
                ins.then_inc(step, 1)
                count[0] += 1
                dve.wait_ge(step, count[0])

            TT, TS, STT = nc.vector.tensor_tensor, nc.vector.tensor_scalar, nc.vector.scalar_tensor_tensor
            dve.wait_ge(loaded, 32)
            dve.wait_ge(scored, 1)
            then(nc.vector.tensor_copy(L[:], scores[:]))
            then(nc.vector.tensor_reduce(m1[:], L[:], AX.X, ALU.max))
            then(TT(s2[:], L[:], over(m1), ALU.is_equal))
            then(TT(s2[:], s2[:], firstb, ALU.mult))
            then(nc.vector.tensor_reduce(r[:], s2[:], AX.X, ALU.max))
            then(TT(one1[:], s2[:], over(r), ALU.is_equal))
            then(TT(s1[:], L[:], over(m1), ALU.subtract))
            then(STT(s2[:], L[:], -1.0, L[:], ALU.mult, ALU.max))
            then(TT(s2[:], s2[:], over(m1), ALU.max))
            then(TT(s3[:], over(m1), L[:], ALU.subtract))
            then(STT(keep[:], s2[:], 0.02, s3[:], ALU.mult, ALU.is_ge))
            dve.wait_ge(exped, 1)
            then(TT(s2[:], s1[:], keep[:], ALU.mult))
            then(nc.vector.tensor_reduce(t[:], s2[:], AX.X, ALU.add))
            then(nc.vector.reciprocal(t[:], t[:]))
            then(TT(wte[:], one1[:], over(t), ALU.mult))
            then(STT(L2[:], one1[:], BIG, L[:], ALU.mult, ALU.add))
            then(nc.vector.tensor_reduce(m2[:], L2[:], AX.X, ALU.max))
            then(TT(s2[:], L2[:], over(m2), ALU.is_equal))
            then(TT(s2[:], s2[:], firstb, ALU.mult))
            then(nc.vector.tensor_reduce(r[:], s2[:], AX.X, ALU.max))
            then(TT(one1[:], s2[:], over(r), ALU.is_equal))
            then(TT(s1[:], L2[:], over(m2), ALU.subtract))
            then(STT(s2[:], L2[:], -1.0, L2[:], ALU.mult, ALU.max))
            then(TT(s2[:], s2[:], over(m2), ALU.max))
            then(TT(s3[:], over(m2), L2[:], ALU.subtract))
            then(STT(keep[:], s2[:], 0.02, s3[:], ALU.mult, ALU.is_ge))
            dve.wait_ge(exped, 2)
            then(TT(s2[:], s1[:], keep[:], ALU.mult))
            then(nc.vector.tensor_reduce(t[:], s2[:], AX.X, ALU.add))
            then(nc.vector.reciprocal(t[:], t[:]))
            then(TT(s2[:], one1[:], over(t), ALU.mult))
            then(TT(wte[:], wte[:], s2[:], ALU.add))


def moe_dense_phase(nc, d, x, xn, wte, eye):
    Q = E * FC
    HIGH, LOW = 0, 1
    PARTS = [(HIGH, HIGH), (HIGH, LOW), (LOW, HIGH)]
    with ExitStack() as ctx:
        sem = lambda s: ctx.enter_context(nc.semaphore(f"moe_{s}"))
        sb = lambda s, shape: ctx.enter_context(nc.sbuf_tensor(f"moe_{s}", shape, F32))
        part = lambda s, shape: ctx.enter_context(nc.sbuf_tensor(f"moe_{s}", shape, F32R))
        ps = lambda s, shape: ctx.enter_context(nc.psum_tensor(f"moe_{s}", shape, F32))
        w1, w3, w2 = (part(s, [P, 2, E, F]) for s in ("w1", "w3", "w2"))
        xp, hp = part("xp", [P, 2, N]), part("hp", [P, 2, 2, N])
        silu, h = sb("silu", [P, 2, N]), sb("h", [P, 2, N])
        raw = [silu[:, 0, :], silu[:, 1, :], h[:, 0, :], h[:, 1, :]]
        RAW = len(raw)
        pick_raw, pick = sb("pick_raw", [2 * E, E]), part("pick", [2 * E, E])
        eye_r = part("eye_r", [P, P])
        weight = part("weight", [P, SUB, 2, E])
        rows = part("rows", [2 * E, N])
        weighted = sb("weighted", [P, N])
        b1, b3, y = ([ps(f"{s}{u}", [P, N]) for u in range(2)] for s in ("b1", "b3", "y"))
        rows_bank = ps("rows_bank", [2 * E, N])
        over = ps("over", [P, N])
        w_loaded, pick_loaded = [sem(f"w_loaded{r}") for r in range(RAW)], sem("pick_loaded")
        w_high, w_split, const_ready = sem("w_high"), sem("w_split"), sem("const")
        x_high, x_split, h_high, h_split = sem("x_high"), sem("x_split"), sem("h_high"), sem("h_split")
        weight_high, weight_split, weight_turned, rows_ready = (sem("weight_high"), sem("weight_split"),
                                                                sem("weight_turned"), sem("rows"))
        gated, upped, silu_ready, h_ready = sem("gated"), sem("upped"), sem("silu"), sem("h")
        y_ready, over_ready, spread, y_weighted, x_added = sem("y"), sem("over"), sem("spread"), sem("y_weighted"), sem("x_added")
        weights = [(w, name, e) for e in range(E) for w, name in ((w1, "w1"), (w3, "w3"), (w2, "w2"))]
        block = ctx.enter_context(nc.Block())

        @block.sync
        def _(sp):
            sp.dma_start(pick_raw[:], d["c_pick"]).then_inc(pick_loaded, 16)
            for k, (w, name, e) in enumerate(weights):
                if k >= RAW:
                    sp.wait_ge(w_split, k - RAW + 1)
                sp.dma_start(raw[k % RAW], d["L0_ffn_" + name][:, e]).then_inc(w_loaded[k % RAW], 16)
            sp.wait_ge(pick_loaded, 16)
            for w in w_loaded:
                sp.wait_ge(w, len(weights) // RAW * 16)

        @block.tensor
        def _(pe):
            pe.wait_ge(w_split, len(weights))
            pe.wait_ge(const_ready, 2)
            with pe.Fori(0, TOK // N) as i:
                def up(bank, w, e, c):
                    for k, (wk, xk) in enumerate(PARTS):
                        last = nc.tensor.matmul(bank[:], w[:, wk, e, c * P:(c + 1) * P], xp[:, xk, :],
                                                start=(k == 0), stop=(k == 2))
                    return last

                def down(q):
                    e, c = divmod(q, FC)
                    pe.wait_ge(h_split, i * Q + q + 1)
                    if c == 0:
                        pe.wait_ge(y_weighted, i * E + e + 1)
                    if c == FC - 1:
                        pe.wait_ge(y_weighted, i * E + e + 2)
                        pe.wait_ge(rows_ready, i + 1)
                        nc.tensor.matmul(over[:], pick[:, e:e + 1].broadcast_to([2 * E, P]), rows[:],
                                         start=True, stop=True).then_inc(over_ready, 1)
                    for k, (hk, wk) in enumerate(PARTS):
                        last = nc.tensor.matmul(y[e % 2][:], w2[:, wk, e, c * P:(c + 1) * P], hp[:, hk, q % 2, :],
                                                start=(c == 0 and k == 0), stop=(c == FC - 1 and k == 2))
                    last.then_inc(y_ready, 1)

                pe.wait_ge(x_split, i + 1)
                for q in range(Q):
                    e, c = divmod(q, FC)
                    pe.wait_ge(silu_ready, i * Q + q + 1)
                    up(b1[q % 2], w1, e, c).then_inc(gated, 1)
                    if q >= 2:
                        pe.wait_ge(h_ready, i * Q + q - 1)
                    up(b3[q % 2], w3, e, c).then_inc(upped, 1)
                    if q == 0:
                        pe.wait_ge(weight_split, i + 1)
                        for t in range(SUB):
                            last = nc.tensor.matmul(rows_bank[:, t * P:(t + 1) * P],
                                                    weight[:, t, :, :].rearrange("p k e -> p (k e)"), eye_r[:],
                                                    start=True, stop=True)
                        last.then_inc(weight_turned, 1)
                    if q >= 2:
                        down(q - 2)
                down(Q - 2)
                down(Q - 1)

        @block.scalar
        def _(act):
            for k, (w, name, e) in enumerate(weights):
                act.wait_ge(w_loaded[k % RAW], (k // RAW + 1) * 16)
                nc.scalar.activation(w[:, HIGH, e, :], raw[k % RAW], ACT.Copy).then_inc(w_high, 1)
            act.sem_inc(silu_ready, 2)
            with act.Fori(0, TOK // N) as i:
                def high(q):
                    act.wait_ge(h_ready, i * Q + q + 1)
                    if q >= 2:
                        act.wait_ge(y_ready, i * Q + q - 1)
                    nc.scalar.activation(hp[:, HIGH, q % 2, :], h[:, q % 2, :], ACT.Copy).then_inc(h_high, 1)

                def copy_over(e):
                    act.wait_ge(over_ready, i * E + e + 1)
                    act.wait_ge(x_added, i * E + e + 1)
                    nc.scalar.activation(weighted[:], over[:], ACT.Copy).then_inc(spread, 1)

                for q in range(Q):
                    act.wait_ge(gated, i * Q + q + 1)
                    if q >= 2:
                        act.wait_ge(h_ready, i * Q + q - 1)
                    nc.scalar.activation(silu[:, q % 2, :], b1[q % 2][:], ACT.Silu).then_inc(silu_ready, 1)
                    if q:
                        high(q - 1)
                    if q > FC and q % FC == 1:
                        copy_over(q // FC - 1)
                    if q == 1:
                        act.wait_ge(weight_turned, i + 1)
                        nc.scalar.activation(rows[:], rows_bank[:], ACT.Copy).then_inc(rows_ready, 1)
                high(Q - 1)
                copy_over(E - 1)

        @block.vector
        def _(dve):
            dve.wait_ge(pick_loaded, 16)
            nc.vector.tensor_copy(pick[:], pick_raw[:]).then_inc(const_ready, 1)
            nc.vector.tensor_copy(eye_r[:], eye[:]).then_inc(const_ready, 1)
            for k, (w, name, e) in enumerate(weights):
                dve.wait_ge(w_high, k + 1)
                nc.vector.tensor_tensor(w[:, LOW, e, :], raw[k % RAW], w[:, HIGH, e, :].bitcast(F32),
                                        ALU.subtract).then_inc(w_split, 1)
            dve.sem_inc(y_weighted, 2)
            dve.sem_inc(x_added, 1)
            with dve.Fori(0, TOK // N) as i:
                xt = xn[:, bass.ds(i * N, N)]
                nc.vector.tensor_copy(xp[:, HIGH, :], xt).then_inc(x_high, 1)
                dve.wait_ge(x_high, i + 1)
                nc.vector.tensor_tensor(xp[:, LOW, :], xt, xp[:, HIGH, :].bitcast(F32), ALU.subtract).then_inc(x_split, 1)
                wt = wte[:, bass.ds(i * SUB, SUB), :]
                nc.vector.tensor_copy(weight[:, :, HIGH, :], wt).then_inc(weight_high, 1)
                dve.wait_ge(weight_high, i + 1)
                nc.vector.tensor_tensor(weight[:, :, LOW, :], wt, weight[:, :, HIGH, :].bitcast(F32),
                                        ALU.subtract).then_inc(weight_split, 1)

                def low(q):
                    dve.wait_ge(h_high, i * Q + q + 1)
                    nc.vector.tensor_tensor(hp[:, LOW, q % 2, :], h[:, q % 2, :], hp[:, HIGH, q % 2, :].bitcast(F32),
                                            ALU.subtract).then_inc(h_split, 1)

                def weigh(e):
                    dve.wait_ge(y_ready, i * Q + (e + 1) * FC)
                    dve.wait_ge(spread, i * E + e + 1)
                    nc.vector.tensor_tensor(weighted[:], y[e % 2][:], weighted[:], ALU.mult).then_inc(y_weighted, 1)

                def add(e):
                    dve.wait_ge(y_weighted, i * E + e + 3)
                    xs = x[:, bass.ds(i * N, N)]
                    nc.vector.tensor_tensor(xs, weighted[:], xs, ALU.add).then_inc(x_added, 1)

                for q in range(Q + 4):
                    if q < Q:
                        dve.wait_ge(silu_ready, i * Q + q + 3)
                        dve.wait_ge(upped, i * Q + q + 1)
                        if q >= 2:
                            dve.wait_ge(h_split, i * Q + q - 1)
                        nc.vector.tensor_tensor(h[:, q % 2, :], b3[q % 2][:], silu[:, q % 2, :],
                                                ALU.mult).then_inc(h_ready, 1)
                    if 1 <= q <= Q:
                        low(q - 1)
                    if q > FC and q % FC == 2:
                        weigh(q // FC - 1)
                    if q > FC and q % FC == 3:
                        add(q // FC - 1)


def rwkv_phase(nc, d, x, center, mean, eye, eps):
    U = 2
    T = SEQ // C
    TH = T * H
    ROUNDS = SEQS // U
    NL = len(LEVELS)
    with ExitStack() as ctx:
        sem = lambda s: ctx.enter_context(nc.semaphore(f"l1a_{s}"))
        sb = lambda s, shape, dt=F32: ctx.enter_context(nc.sbuf_tensor(f"l1a_{s}", shape, dt))
        bank = [[ctx.enter_context(nc.psum_tensor(f"l1a_bank{u}{b}", [P, N], F32)) for b in range(4)] for u in range(U)]
        w1, w2a, w2b = sb("w1", [P, MIX * 32]), sb("w2a", [P, P]), sb("w2b", [32, P])
        rW, kW, vW, oW = sb("rW", [P, H, DK]), sb("kW", [P, H, DK]), sb("vW", [P, P]), sb("oW", [P, P])
        wA, wB, gA, gB = sb("wA", [P, LR]), sb("wB", [LR, H, DK]), sb("gA", [P, LR]), sb("gB", [LR, P])
        cols = sb("cols", [P, 17])
        x_bias, w_b, bonus = cols[:, 0:5], cols[:, 5:9], cols[:, 9:13]
        mu, g_b, gn_w, gn_b = (cols[:, j:j + 1] for j in range(13, 17))
        half_gb = sb("half_gb", [P, 1])
        masks = sb("masks", [P, NL, C], I32)
        square, logvar, rstd = (sb(s, [P, U, N]) for s in ("square", "logvar", "rstd"))
        xn, delta, scaled, z_last = (sb(s, [P, U, N]) for s in ("xn", "delta", "scaled", "z_last"))
        low, low4, lowrank = sb("low", [P, U, N]), sb("low4", [32, U, N]), sb("lowrank", [LR, U, N])
        q, k, decay, uq, S = (sb(s, [P, U, T, H, C]) for s in ("q", "k", "decay", "uq", "S"))
        v = sb("v", [P, U, T, P])
        state = sb("state", [P, U, T - 1, H, DV])
        g, silu_g, o = (sb(s, [P, U, N]) for s in ("g", "silu_g", "o"))
        flat = lambda t, u: t[:, u, :, :, :].rearrange("p t h c -> p (t h c)")
        z = lambda u, m: flat(S, u)[:, m * N:(m + 1) * N] if m < 4 else z_last[:, u, :]
        kT = uq

        def halves(t, u, p, h):
            return flat(t, u)[:, p * (TH * C // 2):(p + 1) * (TH * C // 2)].rearrange("p (n two h) -> p n two h", two=2, h=h)

        loaded, prepared = sem("loaded"), sem("prepared")
        centered_ready, square_ready, var_ready, log_ready, rstd_ready = (
            sem(s) for s in ("centered", "square", "var", "log", "rstd"))
        xn_ready, delta_ready, z0_ready = sem("xn"), sem("delta"), sem("z0")
        low_mm, low4_mm, low_ready, low4_ready, x5_ready = sem("low_mm"), sem("low4_mm"), sem("low"), sem("low4"), sem("x5")
        mix_scaled, mix_ready = sem("mix_scaled"), sem("mix")
        r_mm, q_ready, uq_ready, k_mm, k_ready = sem("r_mm"), sem("q"), sem("uq"), sem("k_mm"), sem("k")
        wA_mm, wA_ready, wB_mm, exp_ready, decay_ready = sem("wA_mm"), sem("wA"), sem("wB_mm"), sem("exp"), sem("decay")
        v_mm, v_ready, gA_mm, gA_ready, gB_mm, g_ready, silu_ready = (
            sem(s) for s in ("v_mm", "v", "gA_mm", "gA", "gB_mm", "g", "silu"))
        diag_mm, diag_ready, level_mm, merged = sem("diag_mm"), sem("diag"), sem("level_mm"), sem("merged")
        q_scaled, k_scaled, total_ready = sem("q_scaled"), sem("k_scaled"), sem("total")
        turned, kT_ready, kv_mm, state_step = sem("turned"), sem("kT"), sem("kv_mm"), sem("state")
        o_mm, o_ready, oc_mm, osquare_ready, ovar_mm, olog_ready, orstd_ready = (
            sem(s) for s in ("o_mm", "o", "oc_mm", "osquare", "ovar_mm", "olog", "orstd"))
        o_step, out_mm, x_added = sem("o_step"), sem("out_mm"), sem("x_added")
        loads = [(w1[:], "xp_W1"), (w2a[:], "xp_W2a"), (w2b[:], "xp_W2b"), (rW[:], "r_W"), (kW[:], "k_W"),
                 (vW[:], "v_W"), (oW[:], "o_W"), (wA[:], "w_A"), (wB[:], "w_B"), (gA[:], "g_A"), (gB[:], "g_B"),
                 (x_bias, "x_bias"), (w_b, "w_b"), (bonus, "bonus"), (mu, "xp_mu"), (g_b, "g_b"),
                 (gn_w, "gn_w"), (gn_b, "gn_b")]
        LOADED = 16 * (len(loads) + 1)
        block = ctx.enter_context(nc.Block())

        @block.sync
        def _(sp):
            for t, s in loads:
                sp.dma_start(t, d["L1_attn_" + s]).then_inc(loaded, 16)
            sp.dma_start(masks[:], d["c_masks"]).then_inc(loaded, 16)
            sp.wait_ge(loaded, LOADED)

        STEPS = NL + 4

        def in_order(eng, core, project):
            def beside(u, r_core, r_project):
                for s in range(STEPS):
                    core(u, s, r_core)
                    project(1 - u, s, r_project)

            for s in range(STEPS):
                project(0, s, 0)
            with eng.Fori(0, ROUNDS - 1) as i:
                beside(0, i, i)
                beside(1, i, i + 1)
            beside(0, ROUNDS - 1, ROUNDS - 1)
            for s in range(STEPS):
                core(1, s, ROUNDS - 1)

        def nth(u, r, per=1, j=0):
            return (r * U + u) * per + (j + 1)

        @block.tensor
        def _(pe):
            pe.wait_ge(loaded, LOADED)
            mm, tr = nc.tensor.matmul, nc.tensor.transpose

            def project(u, s, r):
                B = bank[u]
                if s == 0:
                    pe.wait_ge(x_added, nth(u, r))
                    mm(B[0][:], center[:], x[:, bass.ds(r * (U * N) + u * N, N)], start=True,
                       stop=True).then_inc(centered_ready, 1)
                elif s == 1:
                    pe.wait_ge(square_ready, nth(u, r))
                    mm(B[1][:], mean[:], square[:, u, :], start=True, stop=True).then_inc(var_ready, 1)
                elif s == 2:
                    pe.wait_ge(z0_ready, nth(u, r))
                    mm(B[2][:], w1[:, 0:P], z_last[:, u, :], start=True, stop=True).then_inc(low_mm, 1)
                    mm(B[3][0:32, :], w1[:, P:P + 32], z_last[:, u, :], start=True, stop=True).then_inc(low4_mm, 1)
                elif s == 3:
                    pe.wait_ge(low_ready, nth(u, r))
                    pe.wait_ge(low4_ready, nth(u, r))
                    for m in range(4):
                        mm(B[m][:], w2a[32 * m:32 * m + 32, :], low[32 * m:32 * m + 32, u, :], start=True,
                           stop=True).then_inc(x5_ready, 1)
                    pe.wait_ge(mix_scaled, nth(u, r, 5, 0))
                    mm(B[0][:], w2b[:], low4[:, u, :], start=True, stop=True).then_inc(x5_ready, 1)
                elif s == 5:
                    pe.wait_ge(mix_ready, nth(u, r, 5, 0))
                    for j in range(H):
                        pe.wait_ge(mix_scaled, nth(u, r, 5, j + 1))
                        mm(B[(j + 1) % 4][:], rW[:, j, :], z(u, 0), start=True, stop=True).then_inc(r_mm, 1)
                elif s == 6:
                    pe.wait_ge(mix_ready, nth(u, r, 5, 1))
                    pe.wait_ge(uq_ready, nth(u, r, H, 0))
                    mm(B[1][0:LR, :], wA[:], z(u, 1), start=True, stop=True).then_inc(wA_mm, 1)
                    pe.wait_ge(mix_ready, nth(u, r, 5, 2))
                    for j in range(H):
                        if j < 3:
                            pe.wait_ge(uq_ready, nth(u, r, H, j + 1))
                        else:
                            pe.wait_ge(wA_ready, nth(u, r))
                        mm(B[(j + 2) % 4][:], kW[:, j, :], z(u, 2), start=True, stop=True).then_inc(k_mm, 1)
                elif s == 7:
                    pe.wait_ge(wA_ready, nth(u, r))
                    for j in range(H):
                        pe.wait_ge(k_ready, nth(u, r, H, j))
                        mm(B[(j + 2) % 4][:], wB[:, j, :], lowrank[:, u, :], start=True, stop=True).then_inc(wB_mm, 1)
                elif s == 8:
                    pe.wait_ge(mix_ready, nth(u, r, 5, 3))
                    pe.wait_ge(exp_ready, nth(u, r, H, 0))
                    for t in range(T):
                        last = mm(B[2][:, t * C:(t + 1) * C], z(u, 3)[:, t * C:(t + 1) * C], vW[:], start=True, stop=True)
                    last.then_inc(v_mm, 1)
                    pe.wait_ge(mix_ready, nth(u, r, 5, 4))
                    pe.wait_ge(exp_ready, nth(u, r, H, 1))
                    mm(B[3][0:LR, :], gA[:], z(u, 4), start=True, stop=True).then_inc(gA_mm, 1)
                elif s == 9:
                    pe.wait_ge(gA_ready, nth(u, r))
                    pe.wait_ge(exp_ready, nth(u, r, H, 2))
                    mm(B[0][:], gB[:], lowrank[:, u, :], start=True, stop=True).then_inc(gB_mm, 1)

            def core(u, s, r):
                B = bank[u]
                if s == 0:
                    for t in range(T):
                        if t == 0:
                            pe.wait_ge(exp_ready, nth(u, r, H, 3))
                        elif t == 1:
                            pe.wait_ge(v_ready, nth(u, r))
                        elif t == 3:
                            pe.wait_ge(g_ready, nth(u, r))
                        for j in range(H):
                            last = mm(B[(t + 1) % 4][:, j * C:(j + 1) * C], k[:, u, t, j, :], uq[:, u, t, j, :],
                                      start=True, stop=True)
                        last.then_inc(diag_mm, 1)
                elif s <= NL:
                    l, h = s - 1, LEVELS[s - 1]
                    for p in range(2):
                        if l:
                            pe.wait_ge(k_scaled, nth(u, r, 2 * NL, 2 * (l - 1) + p))
                            pe.wait_ge(q_scaled, nth(u, r, 2 * NL, 2 * (l - 1) + p))
                        b = (2 * (l % 2) + p + 1) % 4
                        if l < 2:
                            pe.wait_ge(diag_ready, nth(u, r, T, 2 * l + p))
                        else:
                            pe.wait_ge(merged, nth(u, r, 2 * NL, 2 * (l - 2) + p))
                        for c in range(2 * H):
                            t, j = 2 * p + c // H, c % H
                            last = mm(B[b][:, c * 64:(c + 1) * 64].rearrange("p (n h) -> p n h", h=h),
                                      k[:, u, t, j, :],
                                      q[:, u, t, j, :].rearrange("p (n two h) -> p n two h", two=2, h=h)[:, :, 1, :],
                                      start=True, stop=True)
                        last.then_inc(level_mm, 1)
                elif s == NL + 1:
                    pe.wait_ge(k_scaled, nth(u, r, 2 * NL, 2 * NL - 1))
                    pe.wait_ge(merged, nth(u, r, 2 * NL, 2 * NL - 1))
                    for t in range(T - 1):
                        for j in range(H):
                            last = tr(B[t + 1][:, j * C:(j + 1) * C], k[:, u, t, j, :], eye[:])
                        last.then_inc(turned, 1)
                    for t in range(T - 1):
                        pe.wait_ge(kT_ready, nth(u, r, T - 1, t))
                        for j in range(H):
                            last = mm(B[0][:, t * P + j * DV:t * P + (j + 1) * DV], kT[:, u, t, j, :],
                                      v[:, u, t, j * DV:(j + 1) * DV], start=True, stop=True)
                        last.then_inc(kv_mm, 1)
                    for t in range(T):
                        if t == 0:
                            pe.wait_ge(q_scaled, nth(u, r, 2 * NL, 2 * NL - 1))
                        else:
                            pe.wait_ge(state_step, nth(u, r, 2 * T - 3, 2 * t - 2))
                        for j in range(H):
                            out = B[1][j * DV:(j + 1) * DV, t * C:(t + 1) * C]
                            last = mm(out, v[:, u, t, j * DV:(j + 1) * DV], S[:, u, t, j, :], start=True, stop=(t == 0))
                            if t:
                                last = mm(out, state[:, u, t - 1, j, :], q[:, u, t, j, :], start=False, stop=True)
                    last.then_inc(o_mm, 1)
                elif s == NL + 2:
                    pe.wait_ge(o_ready, nth(u, r))
                    mm(B[2][:], center[:], o[:, u, :], start=True, stop=True).then_inc(oc_mm, 1)
                    pe.wait_ge(osquare_ready, nth(u, r))
                    mm(B[3][:], mean[:], square[:, u, :], start=True, stop=True).then_inc(ovar_mm, 1)
                elif s == NL + 3:
                    pe.wait_ge(o_step, nth(u, r, 3, 2))
                    mm(B[0][:], oW[:], o[:, u, :], start=True, stop=True).then_inc(out_mm, 1)

            in_order(pe, core, project)

        @block.scalar
        def _(act):
            A = nc.scalar.activation
            act.wait_ge(loaded, LOADED)
            act.wait_ge(prepared, 1)
            chunks = lambda b: b.rearrange("p (t c) -> p t c", c=C)

            def project(u, s, r):
                B = bank[u]
                if s == 0:
                    act.wait_ge(centered_ready, nth(u, r))
                    A(square[:, u, :], B[0][:], ACT.Square).then_inc(square_ready, 1)
                elif s == 1:
                    act.wait_ge(var_ready, nth(u, r))
                    A(logvar[:, u, :], B[1][:], ACT.Ln, bias=eps[:, 0:1]).then_inc(log_ready, 1)
                    act.wait_ge(log_ready, nth(u, r))
                    A(rstd[:, u, :], logvar[:, u, :], ACT.Exp, scale=-0.5).then_inc(rstd_ready, 1)
                elif s == 2:
                    act.wait_ge(low_mm, nth(u, r))
                    A(low[:, u, :], B[2][:], ACT.Tanh).then_inc(low_ready, 1)
                    act.wait_ge(low4_mm, nth(u, r))
                    A(low4[:, u, :], B[3][0:32, :], ACT.Tanh).then_inc(low4_ready, 1)
                elif s == 5:
                    for j in range(H):
                        act.wait_ge(r_mm, nth(u, r, H, j))
                        A(q[:, u, :, j, :], chunks(B[(j + 1) % 4][:]), ACT.Copy).then_inc(q_ready, 1)
                        A(uq[:, u, :, j, :], chunks(B[(j + 1) % 4][:]), ACT.Copy,
                          scale=bonus[:, j:j + 1]).then_inc(uq_ready, 1)
                elif s == 6:
                    act.wait_ge(wA_mm, nth(u, r))
                    A(lowrank[:, u, :], B[1][0:LR, :], ACT.Tanh).then_inc(wA_ready, 1)
                    for j in range(H):
                        act.wait_ge(k_mm, nth(u, r, H, j))
                        A(k[:, u, :, j, :], chunks(B[(j + 2) % 4][:]), ACT.Copy).then_inc(k_ready, 1)
                elif s == 7:
                    for j in range(H):
                        act.wait_ge(wB_mm, nth(u, r, H, j))
                        A(decay[:, u, :, j, :], chunks(B[(j + 2) % 4][:]), ACT.Exp,
                          bias=w_b[:, j:j + 1]).then_inc(exp_ready, 1)
                elif s == 8:
                    act.wait_ge(v_mm, nth(u, r))
                    A(v[:, u, :, :], chunks(B[2][:]), ACT.Copy).then_inc(v_ready, 1)
                    for j in range(H):
                        act.wait_ge(exp_ready, nth(u, r, H, j))
                        A(decay[:, u, :, j, :], decay[:, u, :, j, :], ACT.Exp, scale=-1.0).then_inc(decay_ready, 1)
                    act.wait_ge(gA_mm, nth(u, r))
                    A(lowrank[:, u, :], B[3][0:LR, :], ACT.Tanh).then_inc(gA_ready, 1)
                elif s == 9:
                    act.wait_ge(gB_mm, nth(u, r))
                    A(silu_g[:, u, :], B[0][:], ACT.Tanh, bias=half_gb[:, 0:1], scale=0.5)
                    A(g[:, u, :], B[0][:], ACT.Identity, bias=g_b).then_inc(g_ready, 1)

            def core(u, s, r):
                B = bank[u]
                if s == NL + 1:
                    for t in range(T - 1):
                        act.wait_ge(turned, nth(u, r, T - 1, t))
                        A(kT[:, u, t, :, :].rearrange("p h c -> p (h c)"), B[t + 1][:], ACT.Copy).then_inc(kT_ready, 1)
                    act.wait_ge(o_mm, nth(u, r))
                    A(o[:, u, :], B[1][:], ACT.Copy).then_inc(o_ready, 1)
                elif s == NL + 2:
                    act.wait_ge(oc_mm, nth(u, r))
                    A(square[:, u, :], B[2][:], ACT.Square).then_inc(osquare_ready, 1)
                    act.wait_ge(ovar_mm, nth(u, r))
                    A(logvar[:, u, :], B[3][:], ACT.Ln, bias=eps[:, 0:1]).then_inc(olog_ready, 1)
                    act.wait_ge(olog_ready, nth(u, r))
                    A(rstd[:, u, :], logvar[:, u, :], ACT.Exp, scale=-0.5).then_inc(orstd_ready, 1)

            in_order(act, core, project)

        @block.vector
        def _(dve):
            TT, TS, STT = nc.vector.tensor_tensor, nc.vector.tensor_scalar, nc.vector.scalar_tensor_tensor
            dve.wait_ge(loaded, LOADED)
            TS(half_gb[:], g_b, 0.5, None, ALU.mult).then_inc(prepared, 1)
            dve.sem_inc(x_added, U)

            def mix(u, m, r):
                dve.wait_ge(x5_ready, nth(u, r, 5, m))
                if m:
                    dve.wait_ge(mix_ready, nth(u, r, 5, m - 1))
                STT(scaled[:, u, :], bank[u][m % 4][:], x_bias[:, m:m + 1], delta[:, u, :], ALU.add,
                    ALU.mult).then_inc(mix_scaled, 1)
                dve.wait_ge(mix_scaled, nth(u, r, 5, m))
                TT(z(u, m), scaled[:, u, :], xn[:, u, :], ALU.add).then_inc(mix_ready, 1)

            def project(u, s, r):
                if s == 1:
                    dve.wait_ge(rstd_ready, nth(u, r))
                    TT(xn[:, u, :], bank[u][0][:], rstd[:, u, :], ALU.mult).then_inc(xn_ready, 1)
                    dve.wait_ge(xn_ready, nth(u, r))
                    TT(delta[:, u, 1:N], xn[:, u, 0:N - 1], xn[:, u, 1:N], ALU.subtract).then_inc(delta_ready, 1)
                    TS(delta[:, u, 0:1], xn[:, u, 0:1], -1.0, None, ALU.mult).then_inc(delta_ready, 1)
                    dve.wait_ge(delta_ready, nth(u, r, 2, 1))
                    STT(z_last[:, u, :], delta[:, u, :], mu, xn[:, u, :], ALU.mult, ALU.add).then_inc(z0_ready, 1)
                elif s in (3, 4):
                    for m in range(2) if s == 3 else range(2, MIX):
                        mix(u, m, r)
                elif s == 10:
                    dve.wait_ge(g_ready, nth(u, r))
                    STT(silu_g[:, u, :], silu_g[:, u, :], 1.0, g[:, u, :], ALU.add, ALU.mult).then_inc(silu_ready, 1)

            def core(u, s, r):
                B = bank[u]
                if s == 0:
                    for t in range(T):
                        dve.wait_ge(diag_mm, nth(u, r, T, t))
                        TT(S[:, u, t, :, :], B[(t + 1) % 4][:].rearrange("p (h c) -> p h c", c=C),
                           broadcast(eye[:], 1, H), ALU.mult).then_inc(diag_ready, 1)
                elif s <= NL:
                    l, h = s - 1, LEVELS[s - 1]
                    for p in range(2):
                        dve.wait_ge(level_mm, nth(u, r, 2 * NL, 2 * l + p))
                        if l:
                            dve.wait_ge(total_ready, nth(u, r, 2 * NL, 2 * (l - 1) + p))
                        elif p == 0:
                            dve.wait_ge(decay_ready, nth(u, r, H, 3))
                            dve.wait_ge(diag_ready, nth(u, r, T, 3))
                        total = halves(decay, u, p, h)[:, :, :, 0]
                        qh, kh = halves(q, u, p, h)[:, :, 1, :], halves(k, u, p, h)[:, :, 0, :]
                        TT(qh, qh, broadcast(total[:, :, 0], 2, h), ALU.mult).then_inc(q_scaled, 1)
                        TT(kh, kh, broadcast(total[:, :, 1], 2, h), ALU.mult).then_inc(k_scaled, 1)
                        dve.wait_ge(q_scaled, nth(u, r, 2 * NL, 2 * l + p))
                        TT(total[:, :, 0], total[:, :, 0], total[:, :, 1], ALU.mult).then_inc(total_ready, 1)
                    for p in range(2):
                        b = (2 * (l % 2) + p + 1) % 4
                        Sp = S[:, u, 2 * p:2 * p + 2, :, :].rearrange("p t h c -> p (t h c)") \
                            .rearrange("p (g n two h) -> p g n two h", g=2 * H, two=2, h=h)[:, :, :, 1, :]
                        mask = masks[:, l, :].rearrange("p (n two h) -> p n two h", two=2, h=h)[:, :, 1, :]
                        nc.vector.copy_predicated(
                            Sp, broadcast(mask, 1, 2 * H),
                            B[b][:].rearrange("p (g n h) -> p g n h", g=2 * H, h=h)).then_inc(merged, 1)
                elif s == NL + 1:
                    kv = lambda t: B[0][:, t * P:(t + 1) * P].rearrange("p (h v) -> p h v", v=DV)
                    per = 2 * T - 3
                    dve.wait_ge(kv_mm, nth(u, r, T - 1, T - 2))
                    nc.vector.tensor_copy(state[:, u, 0, :, :], kv(0)).then_inc(state_step, 1)
                    for t in range(1, T - 1):
                        dve.wait_ge(state_step, nth(u, r, per, 2 * t - 2))
                        if t == 1:
                            dve.wait_ge(total_ready, nth(u, r, 2 * NL, 2 * NL - 1))
                        TT(state[:, u, t, :, :], state[:, u, t - 1, :, :],
                           broadcast(decay[:, u, t, :, 0], 2, DV), ALU.mult).then_inc(state_step, 1)
                        dve.wait_ge(state_step, nth(u, r, per, 2 * t - 1))
                        TT(state[:, u, t, :, :], kv(t), state[:, u, t, :, :], ALU.add).then_inc(state_step, 1)
                elif s == NL + 2:
                    dve.wait_ge(orstd_ready, nth(u, r))
                    TT(o[:, u, :], B[2][:], rstd[:, u, :], ALU.mult).then_inc(o_step, 1)
                    dve.wait_ge(o_step, nth(u, r, 3, 0))
                    TS(o[:, u, :], o[:, u, :], gn_w, gn_b, ALU.mult, ALU.add).then_inc(o_step, 1)
                    dve.wait_ge(o_step, nth(u, r, 3, 1))
                    dve.wait_ge(silu_ready, nth(u, r))
                    STT(o[:, u, :], o[:, u, :], 0.5, silu_g[:, u, :], ALU.mult, ALU.mult).then_inc(o_step, 1)
                elif s == NL + 3:
                    dve.wait_ge(out_mm, nth(u, r))
                    xs = x[:, bass.ds(r * (U * N) + u * N, N)]
                    TT(xs, B[0][:], xs, ALU.add).then_inc(x_added, 1)

            in_order(dve, core, project)

def fp4_ffn_phase(nc, d, x, xn, eye):
    U = 2
    NX = N // QB
    NH = SUB * I // QB
    IC = [P, P, I - 2 * P]
    NHH = NH // 2
    NW = (6 * P + I) // QB
    with ExitStack() as ctx:
        sem = lambda s: ctx.enter_context(nc.semaphore(f"ffn_{s}"))
        sb = lambda s, shape, dt=F32: ctx.enter_context(nc.sbuf_tensor(f"ffn_{s}", shape, dt))
        bank = [[ctx.enter_context(nc.psum_tensor(f"ffn_bank{u}{b}", [P, N], F32)) for b in range(4)] for u in range(U)]
        w_raw = sb("w_raw", [P, NW, QB])
        unmagic = sb("unmagic", [P, 1])
        w_in = sb("w_in", [P, 2, I])
        w_down = sb("w_down", [P, 3, P])
        xt, xT = sb("xt", [P, U, N]), sb("xT", [P, U, NX, QB])
        xq = sb("xq", [P, U, N])
        silu = sb("silu", [P, U, 2, I])
        h = sb("h", [P, U, NH, QB])
        hq = sb("hq", [P, U, 3, N])
        amax, scale, inv = (sb(s, [P, U, NH]) for s in ("amax", "scale", "inv"))
        v, a = sb("v", [P, U, NH, QB]), sb("a", [P, U, NH, QB])
        low, c = sb("low", [P, U, NH, QB]), sb("c", [P, U, NH, QB])
        loaded, zeroed, unmagic_set = sem("loaded"), sem("zeroed"), sem("unmagic")
        amax_ready, scale_ready, inv_ready, low_step, c_ready, low_ready, rest_ready, high_ready, rounded = (
            sem(s) for s in ("amax", "scale", "inv", "low_step", "c", "low", "rest", "high", "rounded"))
        scaled, magnitude, signed, quantised = sem("scaled"), sem("magnitude"), sem("signed"), sem("quantised")
        w_turned, w_placed = sem("w_turned"), sem("w_placed")
        xt_ready, x_turned, xT_ready, xq_turned, xq_ready = sem("xt"), sem("x_turned"), sem("xT"), sem("xq_turned"), sem("xq")
        gate_up, silu_ready, h_ready, h_turned, hq_ready = sem("gate_up"), sem("silu"), sem("h"), sem("h_turned"), sem("hq")
        down_ready, x_added = sem("down"), sem("x_added")
        ROUNDS = SEQS // U
        mask_sign = -2147483648

        def q_vector(dve, *jobs, meanwhile=None):
            work = []
            for src, u, nb, k, dst in jobs:
                full = [t[:, u, 0:nb, :] for t in (v, a, c, low)]
                work.append((src, dst, k, amax[:, u, 0:nb], scale[:, u, 0:nb], inv[:, u, 0:nb], *full))
            for src, dst, k, amx, scl, inb, vv, aa, cc, ll in work:
                nc.vector.tensor_reduce(amx, src, AX.X, ALU.max, apply_absolute_value=True).then_inc(amax_ready, 1)
            for src, dst, k, amx, scl, inb, vv, aa, cc, ll in work:
                dve.wait_ge(amax_ready, k + 1)
                nc.vector.tensor_scalar(scl, amx, 1.0 / 6.0, 1e-12, ALU.mult, ALU.max).then_inc(scale_ready, 1)
            for src, dst, k, amx, scl, inb, vv, aa, cc, ll in work:
                dve.wait_ge(scale_ready, k + 1)
                nc.vector.reciprocal(inb, scl).then_inc(inv_ready, 1)
            for src, dst, k, amx, scl, inb, vv, aa, cc, ll in work:
                dve.wait_ge(inv_ready, k + 1)
                nc.vector.tensor_tensor(vv, src, broadcast(inb, 2, QB), ALU.mult).then_inc(scaled, 1)
            for src, dst, k, amx, scl, inb, vv, aa, cc, ll in work:
                dve.wait_ge(magnitude, k + 1)
                nc.vector.tensor_scalar(ll, aa, 1.0, MAGIC, ALU.min, ALU.add).then_inc(low_step, 1)
                nc.vector.tensor_scalar(cc, aa, 1.0, SPLIT, ALU.max, ALU.mult).then_inc(c_ready, 1)
            for src, dst, k, amx, scl, inb, vv, aa, cc, ll in work:
                dve.wait_ge(c_ready, k + 1)
                nc.vector.scalar_tensor_tensor(aa, aa, 1.0, cc, ALU.max, ALU.subtract).then_inc(rest_ready, 1)
            if meanwhile:
                meanwhile()
            for src, dst, k, amx, scl, inb, vv, aa, cc, ll in work:
                dve.wait_ge(rest_ready, k + 1)
                nc.vector.tensor_tensor(cc, cc, aa, ALU.add).then_inc(high_ready, 1)
            for src, dst, k, amx, scl, inb, vv, aa, cc, ll in work:
                dve.wait_ge(low_ready, k + 1)
                dve.wait_ge(high_ready, k + 1)
                nc.vector.tensor_tensor(cc, cc, ll, ALU.add).then_inc(rounded, 1)
            for src, dst, k, amx, scl, inb, vv, aa, cc, ll in work:
                dve.wait_ge(rounded, k + 1)
                nc.vector.scalar_tensor_tensor(cc.bitcast(I32), vv.bitcast(I32), mask_sign, cc.bitcast(I32),
                                               ALU.bitwise_and, ALU.bitwise_or).then_inc(signed, 1)
            for src, dst, k, amx, scl, inb, vv, aa, cc, ll in work:
                dve.wait_ge(signed, k + 1)
                nc.vector.tensor_tensor(dst, cc, broadcast(scl, 2, QB), ALU.mult).then_inc(quantised, 1)

        def q_scalar(act, u, nb, k):
            act.wait_ge(scaled, k + 1)
            nc.scalar.activation(a[:, u, 0:nb, :], v[:, u, 0:nb, :], ACT.Abs, scale=NUDGE).then_inc(magnitude, 1)

        def q_low(act, u, nb, k):
            act.wait_ge(low_step, k + 1)
            nc.scalar.activation(low[:, u, 0:nb, :], low[:, u, 0:nb, :], ACT.Identity,
                                 bias=unmagic[:, 0:1]).then_inc(low_ready, 1)

        block = ctx.enter_context(nc.Block())

        @block.sync
        def _(sp):
            sp.wait_ge(zeroed, 1)
            wr = w_raw[:].rearrange("p b q -> p (b q)")
            for m, s in enumerate(["w_gate", "w_up"]):
                for r, rows in enumerate(IC):
                    sp.dma_start(wr[0:rows, (3 * m + r) * P:(3 * m + r + 1) * P],
                                 d["L1_ffn_" + s][r * P:r * P + rows, :]).then_inc(loaded, 16)
            sp.dma_start(wr[:, 6 * P:6 * P + I], d["L1_ffn_w_down"]).then_inc(loaded, 16)
            sp.wait_ge(loaded, 7 * 16)

        @block.gpsimd
        def _(pool):
            nc.gpsimd.memset(w_raw[:], 0.0).then_inc(zeroed, 1)
            nc.gpsimd.memset(unmagic[:], -MAGIC - 1.0).then_inc(unmagic_set, 1)

        def in_order(eng, weights, enter, beside, leave):
            R = ROUNDS
            weights()
            enter(0, 0, 1)
            beside(1, 0, 0, 0, 2, 1)
            with eng.Fori(0, R - 2) as i:
                beside(0, i + 1, 1, i, i * 6 + 5, i + 1)
                beside(1, i + 1, 0, i + 1, i * 6 + 8, i + 2)
            beside(0, R - 1, 1, R - 2, 6 * R - 7, R - 1)
            beside(1, R - 1, 0, R - 1, 6 * R - 4, None)
            leave(1, R - 1, 6 * R - 1)

        def nth(u, r, per=1, j=0):
            return (r * U + u) * per + (j + 1)

        @block.vector
        def _(dve):
            def weights():
                dve.wait_ge(loaded, 7 * 16)
                q_vector(dve, (w_raw[:], 0, NW, 0, w_raw[:]))
                for m in range(2):
                    dve.wait_ge(w_turned, m + 1)
                    nc.vector.tensor_copy(w_in[:, m, :], bank[0][m][:, 0:I]).then_inc(w_placed, 1)
                dve.wait_ge(w_turned, 3)
                for r, rows in enumerate(IC):
                    nc.vector.tensor_copy(w_down[0:rows, r, :], bank[0][2][0:rows, r * P:(r + 1) * P]).then_inc(w_placed, 1)

            def input_job(u, q):
                return xT[:, u, :, :], u, NX, q, xT[:, u, :, :]

            def hidden_job(u, half, q):
                hh = h[:, u, half * NHH:(half + 1) * NHH, :]
                return hh, u, NHH, q, hh

            def hidden(u, r, ts):
                for t in ts:
                    dve.wait_ge(silu_ready, nth(u, r, SUB, t))
                    hrow = h[:, u, t * (I // QB):(t + 1) * (I // QB), :].rearrange("p b q -> p (b q)")
                    nc.vector.tensor_tensor(hrow, bank[u][2 * (t % 2) + 1][:, 0:I], silu[:, u, t % 2, :],
                                            ALU.mult).then_inc(h_ready, 1)

            def add(u, r):
                dve.wait_ge(down_ready, nth(u, r))
                xs = x[:, bass.ds(r * (U * N) + u * N, N)]
                nc.vector.tensor_tensor(xs, bank[u][3][:], xs, ALU.add).then_inc(x_added, 1)

            def enter(u, r, q):
                dve.sem_inc(x_added, U)
                dve.wait_ge(xT_ready, nth(u, r))
                q_vector(dve, input_job(u, q))
                hidden(u, r, range(SUB))

            def beside(v, rv, u, ru, q, ahead):
                dve.wait_ge(xT_ready, nth(v, rv))
                dve.wait_ge(h_ready, nth(u, ru, SUB, 1))
                q_vector(dve, input_job(v, q), hidden_job(u, 0, q + 1))
                if not isinstance(rv, int) or rv:
                    add(v, rv - 1)
                dve.wait_ge(h_ready, nth(u, ru, SUB, 3))
                q_vector(dve, hidden_job(u, 1, q + 2), meanwhile=lambda: hidden(v, rv, [0, 1]))
                hidden(v, rv, [2, 3])

            def leave(u, r, q):
                for half in range(2):
                    dve.wait_ge(h_ready, nth(u, r, SUB, 2 * half + 1))
                    q_vector(dve, hidden_job(u, half, q + half))
                add(1 - u, r)
                add(u, r)

            in_order(dve, weights, enter, beside, leave)

        @block.scalar
        def _(act):
            def input_copied(u, r):
                nc.scalar.activation(xt[:, u, :], xn[:, bass.ds(r * (U * N) + u * N, N)], ACT.Copy).then_inc(xt_ready, 1)

            def input_placed(u, r):
                act.wait_ge(x_turned, nth(u, r))
                nc.scalar.activation(xT[:, u, :, :].rearrange("p b q -> p (b q)"), bank[u][3][:],
                                     ACT.Copy).then_inc(xT_ready, 1)

            def quantised_turned(u, r):
                act.wait_ge(xq_turned, nth(u, r))
                nc.scalar.activation(xq[:, u, :], bank[u][1][:], ACT.Copy).then_inc(xq_ready, 1)

            def silus(u, r, ts):
                for t in ts:
                    act.wait_ge(gate_up, nth(u, r, SUB, t))
                    if t >= 2:
                        act.wait_ge(h_ready, nth(u, r, SUB, t - 2))
                    nc.scalar.activation(silu[:, u, t % 2, :], bank[u][2 * (t % 2)][:, 0:I], ACT.Silu).then_inc(silu_ready, 1)

            def hidden_turned(u, r, half):
                part = slice(half * N // 2, (half + 1) * N // 2)
                for c, rows in enumerate(IC):
                    act.wait_ge(h_turned, nth(u, r, 6, 3 * half + c))
                    nc.scalar.activation(hq[0:rows, u, c, part], bank[u][c][0:rows, part], ACT.Copy).then_inc(hq_ready, 1)

            def enter(u, r, q):
                for s in range(U):
                    input_copied(s, r)
                    input_placed(s, r)
                q_scalar(act, u, NX, q)
                q_low(act, u, NX, q)
                quantised_turned(u, r)
                silus(u, r, range(SUB))

            def beside(v, rv, u, ru, q, ahead):
                if ahead is not None:
                    input_copied(u, ahead)
                q_scalar(act, v, NX, q)
                q_scalar(act, u, NHH, q + 1)
                q_low(act, v, NX, q)
                q_low(act, u, NHH, q + 1)
                if ahead is not None:
                    input_placed(u, ahead)
                quantised_turned(v, rv)
                q_scalar(act, u, NHH, q + 2)
                q_low(act, u, NHH, q + 2)
                silus(v, rv, [0, 1])
                hidden_turned(u, ru, 0)
                silus(v, rv, [2, 3])
                hidden_turned(u, ru, 1)

            def leave(u, r, q):
                for half in range(2):
                    q_scalar(act, u, NHH, q + half)
                    q_low(act, u, NHH, q + half)
                    hidden_turned(u, r, half)

            def weights():
                act.wait_ge(unmagic_set, 1)
                q_scalar(act, 0, NW, 0)
                q_low(act, 0, NW, 0)

            in_order(act, weights, enter, beside, leave)

        @block.tensor
        def _(pe):
            def weights():
                pe.wait_ge(quantised, 1)
                wr = w_raw[:].rearrange("p b q -> p (b q)")
                for m in range(2):
                    for r, rows in enumerate(IC):
                        last = nc.tensor.transpose(bank[0][m][:, r * P:r * P + rows],
                                                   wr[0:rows, (3 * m + r) * P:(3 * m + r + 1) * P], eye[0:rows, 0:rows])
                    last.then_inc(w_turned, 1)
                for r, rows in enumerate(IC):
                    last = nc.tensor.transpose(bank[0][2][0:rows, r * P:(r + 1) * P],
                                               wr[:, 6 * P + r * P:6 * P + r * P + rows], eye[:])
                last.then_inc(w_turned, 1)
                pe.wait_ge(w_placed, 5)

            def turn_input(u, r):
                pe.wait_ge(xt_ready, nth(u, r))
                for t in range(SUB):
                    last = nc.tensor.transpose(bank[u][3][:, t * P:(t + 1) * P], xt[:, u, t * P:(t + 1) * P], eye[:])
                last.then_inc(x_turned, 1)

            def turn_quantised(u, r, q):
                pe.wait_ge(quantised, q + 1)
                xTu = xT[:, u, :, :].rearrange("p b q -> p (b q)")
                for t in range(SUB):
                    last = nc.tensor.transpose(bank[u][1][:, t * P:(t + 1) * P], xTu[:, t * P:(t + 1) * P], eye[:])
                last.then_inc(xq_turned, 1)

            def gate_and_up(u, r, ts):
                for t in ts:
                    pe.wait_ge(xq_ready, nth(u, r))
                    if t == 1:
                        pe.wait_ge(x_added, nth(u, r))
                    if t >= 2:
                        pe.wait_ge(h_ready, nth(u, r, SUB, t - 2))
                    for m in range(2):
                        last = nc.tensor.matmul(bank[u][2 * (t % 2) + m][:, 0:I], xq[:, u, t * P:(t + 1) * P], w_in[:, m, :],
                                                start=True, stop=True)
                    last.then_inc(gate_up, 1)

            def turn_hidden(u, r, half, q):
                pe.wait_ge(quantised, q + 1)
                hu = h[:, u, :, :].rearrange("p b q -> p (b q)")
                for c, rows in enumerate(IC):
                    if half:
                        pe.wait_ge(hq_ready, nth(u, r, 6, c))
                    for t in (2 * half, 2 * half + 1):
                        last = nc.tensor.transpose(bank[u][c][0:rows, t * P:(t + 1) * P],
                                                   hu[:, t * I + c * P:t * I + c * P + rows], eye[:])
                    last.then_inc(h_turned, 1)

            def down(u, r, ahead):
                pe.wait_ge(hq_ready, nth(u, r, 6, 5))
                if ahead is not None:
                    pe.wait_ge(xT_ready, nth(u, ahead))
                for c, rows in enumerate(IC):
                    last = nc.tensor.matmul(bank[u][3][:], w_down[0:rows, c, :], hq[0:rows, u, c, :],
                                            start=(c == 0), stop=(c == 2))
                last.then_inc(down_ready, 1)

            def enter(u, r, q):
                for s in range(U):
                    turn_input(s, r)
                turn_quantised(u, r, q)
                gate_and_up(u, r, range(SUB))

            def beside(v, rv, u, ru, q, ahead):
                if ahead is not None:
                    pe.wait_ge(h_ready, nth(u, ru, SUB, 3))
                    turn_input(u, ahead)
                turn_quantised(v, rv, q)
                gate_and_up(v, rv, [0, 1])
                turn_hidden(u, ru, 0, q + 1)
                gate_and_up(v, rv, [2, 3])
                turn_hidden(u, ru, 1, q + 2)
                down(u, ru, ahead)

            def leave(u, r, q):
                for half in range(2):
                    turn_hidden(u, r, half, q + half)
                down(u, r, None)

            in_order(pe, weights, enter, beside, leave)

def host_layout(inputs):
    a = {k: np.asarray(v) for k, v in inputs.items()}
    t = {"x": a["L0_attn_x"].reshape(TOK, P).T}
    for s in ("Wg_w", "Wr_w", "Wk_w", "Wv_w", "Wo_w"):
        t["L0_attn_" + s] = a["L0_attn_" + s].T
    for s in ("Wg_b", "Wr_b", "Wk_b", "Wv_b", "Wo_b", "mg", "mr", "mk", "mv", "w", "u"):
        t["L0_attn_" + s] = a["L0_attn_" + s].reshape(P, 1)
    t["L0_ffn_gate_w"] = a["L0_ffn_gate_w"].T
    t["L0_ffn_w1"] = a["L0_ffn_w1"].transpose(2, 0, 1)
    t["L0_ffn_w3"] = a["L0_ffn_w3"].transpose(2, 0, 1)
    t["L0_ffn_w2"] = a["L0_ffn_w2"].reshape(E, P, FC, P).transpose(3, 0, 2, 1).reshape(P, E, F)
    for s in ("w_gate", "w_up", "w_down"):
        t["L1_ffn_" + s] = a["L1_ffn_" + s]
    L = lambda s: a["L1_attn_" + s]
    for s in ("xp_W1", "v_W", "o_W", "w_A", "g_A", "g_B", "x_bias", "bonus"):
        t["L1_attn_" + s] = L(s).T
    t["L1_attn_xp_W2a"], t["L1_attn_xp_W2b"] = L("xp_W2").T[:P], L("xp_W2").T[P:]
    for s in ("r_W", "k_W"):
        t["L1_attn_" + s] = L(s).T.reshape(P, H, DK)
    t["L1_attn_w_B"] = L("w_B").T.reshape(LR, H, DK)
    t["L1_attn_w_b"] = L("w_b").reshape(H, DK).T
    for s in ("xp_mu", "g_b", "gn_w", "gn_b"):
        t["L1_attn_" + s] = L(s).reshape(P, 1)
    return t


def kernel(**inputs):
    import concourse.bacc as bacc
    from concourse.bass_utils import run_bass_kernel_spmd as run

    nc = bacc.Bacc("TRN2", target_bir_lowering=False, num_devices=1)
    arrays, d = {}, {}
    for name, a in {**host_layout(inputs), **constants()}.items():
        a = np.ascontiguousarray(a)
        arrays[f"in_{name}"] = a
        d[name] = nc.dram_tensor(f"in_{name}", a.shape, mybir.dt.from_np(a.dtype), kind="ExternalInput").ap()
    out = nc.dram_tensor("out_x", (P, TOK), F32, kind="ExternalOutput").ap()
    build(nc, d, out)
    r = run(nc, [arrays], core_ids=[0])
    return np.ascontiguousarray(r.results[0]["out_x"].T).reshape(SEQS, SEQ, P)
```
